# Optimizing a Trainium2 kernel written in Bass

```python
import numpy as np
import jax
import jax.numpy as jnp

def _softmax(x, axis=-1):
    return jax.nn.softmax(x, axis=axis)

def _gelu(x):
    return jax.nn.gelu(x, approximate=True)

def _silu(x):
    return jax.nn.silu(x)

def _sigmoid(x):
    return jax.nn.sigmoid(x)

def _layernorm(x, axis=-1, eps=1e-05):
    m = jnp.mean(x, axis=axis, keepdims=True)
    v = jnp.var(x, axis=axis, keepdims=True)
    return (x - m) / jnp.sqrt(v + eps)

def _scatter_add(tgt, idx, src, axis=0):
    return tgt.at[idx].add(src)

def _segment_sum(src, seg, n):
    return jax.ops.segment_sum(src, seg, n)
kernel_name = 'mk_conv_seq_d2_conv_nchw512_r2_33354e'

def setup_inputs(seed: int=0):
    np.random.seed(seed)
    _w = jnp.asarray

    def _rec_inputs():
        import jax
        import jax.numpy as jnp
        _gk = jax.random.key(seed)
        x = -0.0003929 + 0.9999 * jax.random.normal(jax.random.fold_in(_gk, 1), (8, 256, 32, 32), jnp.float32)
        return x
    x = _rec_inputs()

    def _L0_conv_setup():
        import jax, jax.numpy as jnp
        import numpy as np
        key = jax.random.key(seed)
        ks = jax.random.split(key, 8)
        B, C, H, W = (8, 256, 32, 32)
        Cq = C // 8
        x = jax.random.normal(ks[0], (B, C, H, W), dtype=jnp.float32)
        s = 1.0 / np.sqrt(C)
        Wq = jax.random.uniform(ks[1], (Cq, C), jnp.float32, -s, s)
        bq = jax.random.uniform(ks[2], (Cq,), jnp.float32, -s, s)
        Wk = jax.random.uniform(ks[3], (Cq, C), jnp.float32, -s, s)
        bk = jax.random.uniform(ks[4], (Cq,), jnp.float32, -s, s)
        Wv = jax.random.uniform(ks[5], (C, C), jnp.float32, -s, s)
        bv = jax.random.uniform(ks[6], (C,), jnp.float32, -s, s)
        gamma = jnp.float32(0.1) * jnp.ones((1,), jnp.float32)
        return {'x': x, 'Wq': Wq, 'bq': bq, 'Wk': Wk, 'bk': bk, 'Wv': Wv, 'bv': bv, 'gamma': gamma}
    _L0_conv_all = _L0_conv_setup()
    _L0_conv_in = {k: v for k, v in _L0_conv_all.items() if k in ('Wq', 'bq', 'Wk', 'bk', 'Wv', 'bv', 'gamma')}
    del _L0_conv_all

    def _L1_conv_setup():
        import jax, jax.numpy as jnp
        import numpy as np
        import math
        GROUPS = 32
        EPS = 1e-05

        def _group_norm(x, w, b):
            B, C, H, W = x.shape
            xr = x.reshape(B, GROUPS, C // GROUPS, H, W)
            mean = xr.mean(axis=(2, 3, 4), keepdims=True)
            var = xr.var(axis=(2, 3, 4), keepdims=True)
            xn = ((xr - mean) * jax.lax.rsqrt(var + EPS)).reshape(B, C, H, W)
            return xn * w[None, :, None, None] + b[None, :, None, None]
        key = jax.random.key(seed)
        ks = jax.random.split(key, 6)
        C = 256
        B, H, W = (4, 32, 32)
        s = 1.0 / math.sqrt(C)
        return {'x': jax.random.normal(ks[0], (B, C, H, W), dtype=jnp.float32), 'norm_w': jnp.ones((C,), jnp.float32), 'norm_b': jnp.zeros((C,), jnp.float32), 'q_w': jax.random.normal(ks[1], (C, C), jnp.float32) * s, 'q_b': jnp.zeros((C,), jnp.float32), 'k_w': jax.random.normal(ks[2], (C, C), jnp.float32) * s, 'k_b': jnp.zeros((C,), jnp.float32), 'v_w': jax.random.normal(ks[3], (C, C), jnp.float32) * s, 'v_b': jnp.zeros((C,), jnp.float32), 'proj_w': jax.random.normal(ks[4], (C, C), jnp.float32) * s, 'proj_b': jnp.zeros((C,), jnp.float32)}
    _L1_conv_all = _L1_conv_setup()
    _L1_conv_in = {k: v for k, v in _L1_conv_all.items() if k in ('norm_w', 'norm_b', 'q_w', 'q_b', 'k_w', 'k_b', 'v_w', 'v_b', 'proj_w', 'proj_b')}
    del _L1_conv_all
    return {'x': x, 'L0_conv_Wq': _L0_conv_in['Wq'], 'L0_conv_bq': _L0_conv_in['bq'], 'L0_conv_Wk': _L0_conv_in['Wk'], 'L0_conv_bk': _L0_conv_in['bk'], 'L0_conv_Wv': _L0_conv_in['Wv'], 'L0_conv_bv': _L0_conv_in['bv'], 'L0_conv_gamma': _L0_conv_in['gamma'], 'L1_conv_norm_w': _L1_conv_in['norm_w'], 'L1_conv_norm_b': _L1_conv_in['norm_b'], 'L1_conv_q_w': _L1_conv_in['q_w'], 'L1_conv_q_b': _L1_conv_in['q_b'], 'L1_conv_k_w': _L1_conv_in['k_w'], 'L1_conv_k_b': _L1_conv_in['k_b'], 'L1_conv_v_w': _L1_conv_in['v_w'], 'L1_conv_v_b': _L1_conv_in['v_b'], 'L1_conv_proj_w': _L1_conv_in['proj_w'], 'L1_conv_proj_b': _L1_conv_in['proj_b']}

def reference(x, L0_conv_Wq, L0_conv_bq, L0_conv_Wk, L0_conv_bk, L0_conv_Wv, L0_conv_bv, L0_conv_gamma, L1_conv_norm_w, L1_conv_norm_b, L1_conv_q_w, L1_conv_q_b, L1_conv_k_w, L1_conv_k_b, L1_conv_v_w, L1_conv_v_b, L1_conv_proj_w, L1_conv_proj_b):
    import jax
    import jax.numpy as jnp

    def _L0_conv_ref(x, Wq, bq, Wk, bk, Wv, bv, gamma):
        import jax, jax.numpy as jnp
        import numpy as np
        B, C, H, W = x.shape
        N = H * W
        xf = x.reshape(B, C, N)
        q = jnp.einsum('oc,bcn->bno', Wq, xf) + bq
        k = jnp.einsum('oc,bcn->bon', Wk, xf) + bk[None, :, None]
        v = jnp.einsum('oc,bcn->bon', Wv, xf) + bv[None, :, None]
        energy = jnp.einsum('bnc,bcm->bnm', q, k)
        attn = jax.nn.softmax(energy, axis=-1)
        out = jnp.einsum('bcj,bij->bci', v, attn).reshape(B, C, H, W)
        return gamma[0] * out + x

    def _L1_conv_ref(x, norm_w, norm_b, q_w, q_b, k_w, k_b, v_w, v_b, proj_w, proj_b):
        import jax, jax.numpy as jnp
        import numpy as np
        import math
        GROUPS = 32
        EPS = 1e-05

        def _group_norm(x, w, b):
            B, C, H, W = x.shape
            xr = x.reshape(B, GROUPS, C // GROUPS, H, W)
            mean = xr.mean(axis=(2, 3, 4), keepdims=True)
            var = xr.var(axis=(2, 3, 4), keepdims=True)
            xn = ((xr - mean) * jax.lax.rsqrt(var + EPS)).reshape(B, C, H, W)
            return xn * w[None, :, None, None] + b[None, :, None, None]
        B, C, H, W = x.shape
        HW = H * W
        h_ = _group_norm(x, norm_w, norm_b).reshape(B, C, HW)
        q = jnp.einsum('oc,bcn->bon', q_w, h_) + q_b[None, :, None]
        k = jnp.einsum('oc,bcn->bon', k_w, h_) + k_b[None, :, None]
        v = jnp.einsum('oc,bcn->bon', v_w, h_) + v_b[None, :, None]
        scale = 1.0 / math.sqrt(C)
        attn = jnp.einsum('bct,bcs->bts', q, k) * scale
        attn = jax.nn.softmax(attn, axis=-1)
        out = jnp.einsum('bcs,bst->bct', v, attn)
        out = jnp.einsum('oc,bcn->bon', proj_w, out) + proj_b[None, :, None]
        return x + out.reshape(B, C, H, W)

    def _gn(v, G=32, eps=1e-05):
        B_, C_, H_, W_ = v.shape
        g = v.reshape(B_, G, C_ // G, H_, W_)
        m = jnp.mean(g, axis=(2, 3, 4), keepdims=True)
        s = jnp.var(g, axis=(2, 3, 4), keepdims=True)
        return ((g - m) / jnp.sqrt(s + eps)).reshape(v.shape)

    def _ln_c(v, eps=1e-06):
        m = jnp.mean(v, axis=1, keepdims=True)
        s = jnp.var(v, axis=1, keepdims=True)
        return (v - m) / jnp.sqrt(s + eps)

    def _ln_t(v, eps=1e-05):
        m = jnp.mean(v, axis=-1, keepdims=True)
        s = jnp.var(v, axis=-1, keepdims=True)
        return (v - m) / jnp.sqrt(s + eps)

    def _to_tokens(v):
        B_, C_, H_, W_ = v.shape
        return v.reshape(B_, C_, H_ * W_).transpose(0, 2, 1)

    def _from_tokens(t, like):
        B_, C_, H_, W_ = like.shape
        return t.transpose(0, 2, 1).reshape(B_, C_, H_, W_)
    x = _L0_conv_ref(x, L0_conv_Wq, L0_conv_bq, L0_conv_Wk, L0_conv_bk, L0_conv_Wv, L0_conv_bv, L0_conv_gamma)
    x = _L1_conv_ref(x, L1_conv_norm_w, L1_conv_norm_b, L1_conv_q_w, L1_conv_q_b, L1_conv_k_w, L1_conv_k_b, L1_conv_v_w, L1_conv_v_b, L1_conv_proj_w, L1_conv_proj_b)
    return x

_drawn_inputs = setup_inputs


def setup_inputs(seed=0):
    import zlib

    import numpy as np

    out = dict(_drawn_inputs(seed))
    spreads = {'L1_conv_norm_w': (1.0, 0.2),
     'L1_conv_norm_b': (0.0, 0.1),
     'L1_conv_q_b': (0.0, 0.429),
     'L1_conv_k_b': (0.0, 0.8),
     'L1_conv_v_b': (0.0, 0.1),
     'L1_conv_proj_b': (0.0, 0.1)}
    factors = {'L0_conv_Wq': 5.179,
     'L0_conv_bq': 8.0,
     'L0_conv_Wk': 5.073,
     'L0_conv_bk': 8.0,
     'L0_conv_Wv': 5.037,
     'L0_conv_bv': 8.0}
    for name, (base, spread) in spreads.items():
        noise = np.random.default_rng([zlib.crc32(name.encode()), seed]).standard_normal(out[name].shape)
        drawn = base * np.exp(spread * noise) if base else spread * noise
        out[name] = jnp.asarray(drawn.astype(out[name].dtype))
    for name, factor in factors.items():
        out[name] = (out[name] * factor).astype(out[name].dtype)
    return out
```

```python
from contextlib import ExitStack

import concourse.bass as bass
from concourse import mybir
from concourse.alu_op_type import AluOpType as ALU

F32 = mybir.dt.float32
F32R = mybir.dt.float32r
ACT = mybir.ActivationFunctionType
AX_X = mybir.AxisListType.X

IMAGES, C, N = 8, 256, 1024
P = 128
CT = C // P
TILES = N // P
HALF = 512
HALVES = N // HALF
PER_HALF = HALF // P
STEPS = 2 * TILES
PV_LAG = 6
GROUP = 8
EPS = 1e-5
QK = 32
VW = C + 2

ITEMS = {
    4: [("query", 0)], 5: [("query", 1)],
    6: [("value1", 0)], 7: [("value1", 1)], 8: [("value1", 2)], 9: [("value1", 3)],
    11: [("qk", 0)], 12: [("qk", 1)],
    14: [("norm", 0), ("value0", 0)], 15: [("norm", 1), ("value0", 1)],
}
IMAGE_OF = {"query": -1, "value1": -1, "qk": 1, "value0": 1, "norm": 0}
AT = {}
for _s in range(STEPS):
    for _x in [("tile", _s)] + ITEMS.get(_s, []):
        AT[_x] = len(AT)
assert len(AT) % 2 == 0

HEAD = [(-1, s) for s in range(11, STEPS)] + [(0, s) for s in range(STEPS)] + [(1, s) for s in range(PV_LAG)]
TURNS = IMAGES - 2
TAIL = ([(IMAGES - 1, s) for s in range(PV_LAG, STEPS)] + [(IMAGES, s) for s in range(STEPS)]
        + [(IMAGES + 1, s) for s in range(PV_LAG)])
BODY = list(range(PV_LAG, STEPS)) + list(range(PV_LAG))

PER_TURN = dict(
    ring_ready=len(AT), row_ready=16, exp_done=16, p_ready=8, p_split=8, t_ready=8, t_hi=8, t_lo=8,
    pv_ready=8, pv_read=8, qk_split=2, query_split=2, value0_split=2, value1_split=4,
    norm_read=2, block0_free=1, proj_hi=10, stats_ready=1, h_split=1, x_split=1, res0_ready=1, res1_ready=1,
    link=38)


class Counts:

    def __init__(self):
        self.n = {name: 0 for name in PER_TURN}
        self.turn = None
        self.marks = {}

    def mark(self, place, name):
        self.marks[place] = (name, self.n[name])

    def up(self, name):
        self.n[name] += 1
        return self.now(name)

    def now(self, name):
        return self.at(name, self.n[name])

    def at(self, name, n):
        return n if self.turn is None else n + self.turn * PER_TURN[name]

    def enter(self, turn):
        self.turn, self.before = turn, dict(self.n)

    def leave(self):
        self.marks = {place: (name, n + (TURNS - 1) * PER_TURN[name] if n > self.before[name] else n)
                      for place, (name, n) in self.marks.items()}
        for name, n in self.n.items():
            if n != self.before[name]:
                assert n - self.before[name] == PER_TURN[name], (name, n - self.before[name])
                self.n[name] += (TURNS - 1) * PER_TURN[name]
        self.turn = None


def tile_before(has, s, back):
    i, t = (0, s - back) if s >= back else (-1, s - back + STEPS)
    layer = t // TILES
    return (layer, t % TILES) if has(i - layer) else None


def eighth(has, s):
    i, t = (0, s - PV_LAG) if s >= PV_LAG else (-1, s - PV_LAG + STEPS)
    layer = t // TILES
    return (layer, t % TILES // 4, t % 4) if has(i - layer) else None


def items(has, s):
    return [(kind, m, AT[kind, m] % 2) for kind, m in ITEMS.get(s, []) if has(IMAGE_OF[kind])]


def run_steps(engine, counts, step):
    for i, s in HEAD:
        step(lambda d: 0 <= i + d < IMAGES, s)
    with engine.Fori(0, TURNS) as turn:
        counts.enter(turn)
        for s in BODY:
            step(lambda d: True, s)
        counts.leave()
    for i, s in TAIL:
        step(lambda d: 0 <= i + d < IMAGES, s)


def build(nc, x, wqk_t, bqk, bk0, wv0_t, bv0, gamma, norm_w, norm_b, wq, bq, wk, bk, wv, bv, wp_t, bp,
          ident, group, y):
    with ExitStack() as ctx:
        def sb(name, shape, dt=F32):
            return ctx.enter_context(nc.sbuf_tensor(name, shape, dt))

        def pair(name, shape):
            return sb(name + "_hi", shape, F32R), sb(name + "_lo", shape, F32R)

        def sem(name):
            return ctx.enter_context(nc.semaphore(name))

        x_in = sb("x_in", [P, CT, N])
        x_hi, x_lo = pair("x", [P, CT, N])
        x1 = sb("x1", [P, CT, N])
        h_f = sb("h_f", [P, 2, HALF])
        h_hi, h_lo = pair("h", [P, CT, N])
        res1 = sb("res1", [P, CT, N])
        query_hi, query_lo = pair("query", [P, CT, N])
        v0_hi, v0_lo = pair("v0", [P, TILES, C])
        v1_hi, v1_lo = pair("v1", [P, TILES, C])
        q4 = sb("q4", [P, N], F32R)
        k4 = sb("k4", [P, N], F32R)
        prob = sb("prob", [P, 2, N])
        pt_hi = [sb(f"pt_hi{j}", [P, TILES, HALF], F32R) for j in range(HALVES)]
        pt_lo = [sb(f"pt_lo{j}", [P, TILES, HALF], F32R) for j in range(HALVES)]
        neg_max = sb("neg_max", [P, 2])
        neg_raw = sb("neg_raw", [P, 2])
        row_sum = sb("row_sum", [P, 2])
        row_inv = sb("row_inv", [P, 2])
        row_const = sb("row_const", [P, TILES])
        bn = sb("bn", [P, CT, HALVES * 6])
        mean_var = sb("mean_var", [P, CT, 2])
        group_mean = sb("group_mean", [P, CT])
        dev = sb("dev", [P, CT])
        dev2 = sb("dev2", [P, CT])
        spread = sb("spread", [P, CT])
        var_eps = sb("var_eps", [P, CT])
        rstd = sb("rstd", [P, CT])
        norm_a = sb("norm_a", [P, CT])
        norm_t = sb("norm_t", [P, CT])
        norm_c = sb("norm_c", [P, CT])
        neg_half = sb("neg_half", [P, CT])
        wq_f, wk_f, wv_f, wp_f = (prob[:, j // 2, (j % 2) * HALF:(j % 2 + 1) * HALF]
                                  .rearrange("p (t c) -> p t c", t=CT) for j in range(4))
        wqk_f = h_f[:, 0, 0:CT * P].rearrange("p (t c) -> p t c", t=CT)
        wv0_f = h_f[:, 1, :].rearrange("p (t c) -> p t c", t=CT)
        wqk_hi, wqk_lo = pair("wqk", [P, CT, P])
        wv0_hi, wv0_lo = pair("wv0", [P, CT, C])
        wqq_hi, wqq_lo = pair("wqq", [P, CT, C])
        wpv_hi, wpv_lo = pair("wpv", [P, CT, VW])
        bqk_s, bk0_s, gamma_s = sb("bqk_s", [P, 1]), sb("bk0_s", [QK, 1]), sb("gamma_s", [P, 1])
        bv0_s, nw_s, nb_s = sb("bv0_s", [P, CT]), sb("nw_s", [P, CT]), sb("nb_s", [P, CT])
        bq_s, bk_s, bv_s, bp_s = (sb(f"{n}_s", [P, CT]) for n in ("bq", "bk", "bv", "bp"))
        gbv = sb("gbv", [P, CT])
        query_b = sb("query_b", [P, CT])
        value_b = sb("value_b", [P, VW], F32R)
        value_bh = sb("value_bh", [1, VW], F32R)
        ones = sb("ones", [P, P], F32R)
        ident_s, group_s = sb("ident_s", [P, P]), sb("group_s", [P, P])

        ring = ctx.enter_context(nc.psum_tensor("ring", [P, 2, N], F32))
        pt_ps = ctx.enter_context(nc.psum_tensor("pt_ps", [P, TILES, P], F32))
        pv_ps = ctx.enter_context(nc.psum_tensor("pv_ps", [P, CT, HALF], F32))
        wqq_ps = pt_ps[:, 0:4, :].rearrange("p a b -> p (a b)").rearrange("p (t c) -> p t c", t=CT)
        wpv_ps = pt_ps[:, 4:8, :].rearrange("p a b -> p (a b)").rearrange("p (t c) -> p t c", t=CT)
        rowk_ps, query_b_ps = (pv_ps[:, 0, 2 * j:2 * j + 2] for j in range(2))
        value_b_ps = pv_ps[0:1, 1, 0:VW]

        S = {name: sem(name) for name in PER_TURN}
        loaded0, loaded1, x_loaded, y_stored = (sem(n) for n in ("loaded0", "loaded1", "x_loaded", "y_stored"))
        ones_ready, bias_ready, wset0, weights_ps, weights_ready = (
            sem(n) for n in ("ones_ready", "bias_ready", "wset0", "weights_ps", "weights_ready"))
        pool_link, x_hi_ready = sem("pool_link"), sem("x_hi_ready")
        pool_passed, dve_passed = sem("pool_passed"), sem("dve_passed")

        def block_of(k):
            return k // PER_HALF, slice(k % PER_HALF * P, (k % PER_HALF + 1) * P)

        block = ctx.enter_context(nc.Block())

        x_v = x.rearrange("b (t p) n -> b p t n", p=P)
        y_v = y.rearrange("b (t p) n -> b p t n", p=P)
        by_tile = lambda w: w.rearrange("(t p) c -> p t c", p=P)

        @block.sync
        def _(sp):
            sp.dma_start(x_in[:], x_v[0]).then_inc(x_loaded, 16)
            for dst, src in ((wqk_f, by_tile(wqk_t)), (wv0_f, by_tile(wv0_t)), (bqk_s[:], bqk), (bk0_s[:], bk0),
                             (gamma_s[:], gamma), (bv0_s[:], bv0), (bq_s[:], bq), (bk_s[:], bk)):
                sp.dma_start(dst, src).then_inc(loaded0, 16)
            for dst, src in ((wq_f, by_tile(wq)), (wk_f, by_tile(wk)), (wv_f, by_tile(wv)), (wp_f, by_tile(wp_t)), (bv_s[:], bv), (bp_s[:], bp),
                             (nw_s[:], norm_w), (nb_s[:], norm_b), (ident_s[:], ident), (group_s[:], group)):
                sp.dma_start(dst, src).then_inc(loaded1, 16)

            def load(i):
                sp.wait_ge(S["res0_ready"], i)
                sp.dma_start(x_in[:], x_v[i]).then_inc(x_loaded, 16)

            def store(b):
                n = b * 8 + 8 if not isinstance(b, int) or b < IMAGES - 1 else b * 8 + 4
                for half in range(HALVES):
                    for ct in range(CT):
                        n = n + 1
                        cols = slice(half * HALF, (half + 1) * HALF)
                        sp.wait_ge(S["pv_read"], n)
                        sp.dma_start(y_v[b][:, ct, cols], res1[:, ct, cols]).then_inc(y_stored, 16)

            load(1)
            with sp.Fori(0, IMAGES - 2) as b:
                load(b + 2)
                store(b)
            store(IMAGES - 2)
            store(IMAGES - 1)
            sp.wait_ge(y_stored, IMAGES * 4 * 16)

        @block.gpsimd
        def _(pool):
            LINKS = 4 + 4 * 2
            links = [0, None]

            def wait(semaphore, n):
                pool.wait_ge(semaphore, n)
                if not isinstance(n, int):
                    pool.sem_inc(pool_passed, 1)

            def link(ins):
                links[0] += 1
                ins.then_inc(pool_link, 1)
                wait(pool_link, links[0] if links[1] is None else links[0] + links[1] * LINKS)

            def split_x(i):
                wait(x_loaded, 16 * (i + 1))
                if not isinstance(i, int) or i > 0:
                    wait(S["value0_split"], 2 * i)
                for ct in range(CT):
                    last = nc.gpsimd.tensor_scalar(x_hi[:, ct], x_in[:, ct], 1.0, None, ALU.mult)
                last.then_inc(x_hi_ready, 1)
                wait(x_hi_ready, i + 1)
                for ct in range(CT):
                    last = nc.gpsimd.tensor_tensor(x_lo[:, ct], x_in[:, ct], x_hi[:, ct].bitcast(F32), ALU.subtract)
                last.then_inc(S["x_split"], 1)

            def normalise(b):
                wait(S["norm_read"], 2 * (b + 1))
                link(nc.gpsimd.tensor_tensor(rstd[:], var_eps[:], neg_half[:], ALU.pow))
                link(nc.gpsimd.tensor_tensor(norm_a[:], rstd[:], nw_s[:], ALU.mult))
                link(nc.gpsimd.tensor_tensor(norm_t[:], group_mean[:], norm_a[:], ALU.mult))
                link(nc.gpsimd.tensor_tensor(norm_c[:], nb_s[:], norm_t[:], ALU.subtract))
                if not isinstance(b, int) or b > 0:
                    wait(S["exp_done"], 16 * b + 8)
                for n in range(4):
                    ct, cols = n % CT, slice(n // CT * HALF, (n // CT + 1) * HALF)
                    link(nc.gpsimd.tensor_scalar(h_f[:, n % 2], x1[:, ct, cols], norm_a[:, ct:ct + 1],
                                                 norm_c[:, ct:ct + 1], ALU.mult, ALU.add))
                    link(nc.gpsimd.tensor_scalar(h_hi[:, ct, cols], h_f[:, n % 2], 1.0, None, ALU.mult))
                    last = nc.gpsimd.tensor_tensor(h_lo[:, ct, cols], h_f[:, n % 2],
                                                   h_hi[:, ct, cols].bitcast(F32), ALU.subtract)
                last.then_inc(S["h_split"], 1)

            def residual1(b):
                if not isinstance(b, int) or b > 0:
                    wait(y_stored, 64 * b)
                for ct in range(CT):
                    last = nc.gpsimd.tensor_scalar(res1[:, ct], x1[:, ct], bp_s[:, ct:ct + 1], None, ALU.add)
                last.then_inc(S["res1_ready"], 1)
                wait(S["res1_ready"], b + 1)

            def residual0(i):
                for ct in range(CT):
                    last = nc.gpsimd.tensor_scalar(x1[:, ct], x_in[:, ct], gbv[:, ct:ct + 1], None, ALU.add)
                last.then_inc(S["res0_ready"], 1)

            nc.gpsimd.memset(ones[:].bitcast(F32), 1.0).then_inc(ones_ready, 1)
            nc.gpsimd.memset(value_b[:].bitcast(F32), 0.0).then_inc(ones_ready, 1)
            nc.gpsimd.memset(neg_half[:], -0.5).then_inc(ones_ready, 1)
            wait(ones_ready, 3)
            split_x(0)
            wait(bias_ready, 1)
            residual0(0)
            split_x(1)
            wait(weights_ready, 1)
            with pool.Fori(0, IMAGES - 2) as b:
                links[1] = b
                normalise(b)
                residual1(b)
                residual0(b + 1)
                split_x(b + 2)
            links[0], links[1] = links[0] + (IMAGES - 3) * LINKS, None
            normalise(IMAGES - 2)
            residual1(IMAGES - 2)
            residual0(IMAGES - 1)
            normalise(IMAGES - 1)
            residual1(IMAGES - 1)

        @block.tensor
        def _(pe):
            c = Counts()
            mm = nc.tensor.matmul

            def wait(name, n):
                pe.wait_ge(S[name], c.at(name, n))

            pe.wait_ge(loaded1, 16 * 10)
            pe.wait_ge(loaded0, 16 * 8)
            for ct in range(CT):
                rows = slice(ct * P, (ct + 1) * P)
                for o in range(CT):
                    mm(wqq_ps[:, ct], wq_f[:, o, rows], wk_f[:, o], start=o == 0, stop=o == CT - 1)
                for o in range(CT):
                    mm(wpv_ps[:, ct], wv_f[:, o, rows], wp_f[:, o], start=o == 0, stop=o == CT - 1)
                for out, w, b in ((rowk_ps, wq_f, bk_s), (query_b_ps, wk_f, bq_s)):
                    for o in range(CT):
                        mm(out[:, ct:ct + 1], w[:, o, rows], b[:, o:o + 1], start=o == 0, stop=o == CT - 1)
            for o in range(CT):
                mm(value_b_ps[:, 0:C], bv_s[:, o:o + 1], wp_f[:, o], start=o == 0, stop=o == CT - 1)
            for j in range(2):
                for o in range(CT):
                    last = mm(value_b_ps[:, C + j:C + j + 1], bq_s[:, o:o + 1], bk_s[:, o:o + 1],
                              start=o == 0, stop=o == CT - 1)
            last.then_inc(weights_ps, 1)
            pe.wait_ge(wset0, 1)

            def three(out, w_hi, w_lo, m_hi, m_lo, first, last):
                mm(out, w_hi, m_hi, start=first, stop=False)
                mm(out, w_hi, m_lo, start=False, stop=False)
                return mm(out, w_lo, m_hi, start=False, stop=last)

            def take(*place):
                if place in c.marks:
                    wait(*c.marks[place])

            def logits(layer, k, slot):
                take("slot", slot)
                rows = slice(k * P, (k + 1) * P)
                if k == 0:
                    name = ("qk_split", "query_split")[layer]
                    wait(name, c.n[name])
                for half in range(HALVES):
                    out = ring[:, slot, half * HALF:(half + 1) * HALF]
                    cols = slice(half * HALF, (half + 1) * HALF)
                    if layer == 0:
                        last = mm(out, q4[:, rows], k4[:, cols], start=True, stop=True)
                    else:
                        for ct in range(CT):
                            last = three(out, query_hi[:, ct, rows], query_lo[:, ct, rows],
                                         h_hi[:, ct, cols], h_lo[:, ct, cols], ct == 0, ct == CT - 1)
                last.then_inc(S["ring_ready"], 1)
                c.up("exp_done")
                c.mark(("slot", slot), "exp_done")

            def transposes(k):
                wait("p_ready", c.n["p_ready"] + 1)
                c.up("p_ready")
                if c.n["t_lo"] or c.turn is not None:
                    wait("t_lo", c.n["t_lo"])
                else:
                    pe.wait_ge(weights_ready, 1)
                for st in range(TILES):
                    last = nc.tensor.transpose(pt_ps[:, st], prob[:, k % 2, st * P:(st + 1) * P], ident_s[:])
                last.then_inc(S["t_ready"], 1)
                c.up("t_lo")

            def values0(half, r, tiles):
                ct = r // 2
                if r == 0:
                    wait("value0_split", c.n["value0_split"])
                    wait("t_lo", tiles)
                if r % 2 == 0:
                    take("bank", ct)
                w = slice(ct * P, (ct + 1) * P)
                for st in range(4 * (r % 2), 4 * (r % 2) + 4):
                    last = three(pv_ps[:, ct], v0_hi[:, st, w], v0_lo[:, st, w], pt_hi[half][:, st],
                                 pt_lo[half][:, st], st == 0, st == TILES - 1)
                if r % 2:
                    last.then_inc(S["pv_ready"], 1)
                    c.up("pv_read")
                    c.mark(("bank", ct), "pv_read")

            def values1(half, r):
                if half == 0:
                    if r == 0:
                        wait("value1_split", c.n["value1_split"])
                    c.up("p_split"), c.up("p_split")
                    wait("p_split", c.n["p_split"])
                for ct in range(CT):
                    if r == 0:
                        take("bank", ct)
                    w = slice(ct * P, (ct + 1) * P)
                    for k in (2 * r, 2 * r + 1):
                        j, cols = block_of(k)
                        keys = slice(half * PER_HALF, (half + 1) * PER_HALF)
                        last = three(pv_ps[:, ct], v1_hi[:, k, w], v1_lo[:, k, w], pt_hi[j][:, keys, cols],
                                     pt_lo[j][:, keys, cols], k == 0, k == TILES - 1)
                    if r == 3:
                        last.then_inc(S["pv_ready"], 1)
                        c.up("pv_read")
                        c.mark(("bank", ct), "pv_read")
                if half == 1 and r == 0:
                    last.then_inc(S["block0_free"], 1)

            def project(kind, m, slot):
                out = ring[:, slot]
                reader = {"norm": "norm_read"}.get(kind, f"{kind}_split")
                if kind == "query":
                    if m == 0:
                        pe.wait_ge(S["h_split"], c.up("h_split"))
                    take("slot", slot)
                    for half in range(HALVES):
                        cols = slice(half * HALF, (half + 1) * HALF)
                        for ct in range(CT):
                            w = (slice(None), ct, slice(m * P, (m + 1) * P))
                            last = three(out[:, cols], wqq_hi[w], wqq_lo[w], h_hi[:, ct, cols],
                                         h_lo[:, ct, cols], ct == 0, ct == CT - 1)
                if kind == "value1":
                    take("slot", slot)
                    for j in range(2):
                        mm(out[:, j * HALF:j * HALF + VW], ones[:], value_b[:], start=True, stop=False)
                        for ct in range(CT):
                            w = (slice(None), ct, slice((2 * m + j) * P, (2 * m + j + 1) * P))
                            last = three(out[:, j * HALF:j * HALF + VW], h_hi[w], h_lo[w], wpv_hi[:, ct],
                                         wpv_lo[:, ct], False, ct == CT - 1)
                if kind == "qk":
                    if m == 0:
                        pe.wait_ge(S["x_split"], c.up("x_split"))
                    take("slot", slot)
                    cols = slice(m * HALF, (m + 1) * HALF)
                    for ct in range(CT):
                        last = three(out[:, 0:HALF], wqk_hi[:, ct], wqk_lo[:, ct], x_hi[:, ct, cols],
                                     x_lo[:, ct, cols], ct == 0, ct == CT - 1)
                if kind == "value0":
                    take("slot", slot)
                    for j in range(4):
                        for ct in range(CT):
                            w = (slice(None), ct, slice((4 * m + j) * P, (4 * m + j + 1) * P))
                            last = three(out[:, j * C:(j + 1) * C], x_hi[w], x_lo[w], wv0_hi[:, ct],
                                         wv0_lo[:, ct], ct == 0, ct == CT - 1)
                if kind == "norm":
                    if m == 0:
                        pe.wait_ge(S["stats_ready"], c.up("stats_ready"))
                    else:
                        wait("norm_read", c.n["norm_read"])
                    take("slot", slot)
                    last = mm(out[:, 0:CT], group_s[:], mean_var[:, :, 0] if m == 0 else spread[:],
                              start=True, stop=True)
                last.then_inc(S["ring_ready"], 1)
                c.up(reader)
                c.mark(("slot", slot), reader)

            def step(has, s):
                if now := tile_before(has, s, 0):
                    logits(*now, AT["tile", s] % 2)
                if part := eighth(has, s):
                    layer, half, r = part
                    if layer == 0:
                        old = tile_before(has, s, 2)
                        values0(half, r, c.n["t_lo"] - bool(old and old[0] == 0))
                    else:
                        values1(half, r)
                for item in items(has, s):
                    project(*item)
                if (old := tile_before(has, s, 1)) and old[0] == 0:
                    transposes(old[1])

            run_steps(pe, c, step)

        @block.scalar
        def _(act):
            c = Counts()
            copy, activation = nc.scalar.copy, nc.scalar.activation

            def step(has, s):
                old = tile_before(has, s, 2)
                if old and old[0] == 0:
                    half, cols = block_of(old[1])
                    if old[1] == 0 and has(-2):
                        act.wait_ge(S["block0_free"], c.up("block0_free"))
                    act.wait_ge(S["t_ready"], c.up("t_ready"))
                    copy(pt_hi[half][:, :, cols], pt_ps[:]).then_inc(S["t_hi"], 1)
                if now := tile_before(has, s, 0):
                    k, slot = now[1], AT["tile", s] % 2
                    act.wait_ge(S["row_ready"], c.up("row_ready"))
                    activation(prob[:, k % 2], ring[:, slot], ACT.Exp, bias=neg_max[:, k % 2:k % 2 + 1],
                               accum_out=row_sum[:, k % 2:k % 2 + 1]).then_inc(S["exp_done"], 1)
                    c.up("ring_ready")
                for kind, m, slot in items(has, s):
                    ready = c.up("ring_ready")
                    if kind == "norm":
                        continue
                    act.wait_ge(S["ring_ready"], ready)
                    out = ring[:, slot]
                    if kind == "query":
                        last = activation(query_hi[:, m], out, ACT.Identity, bias=query_b[:, m:m + 1])
                    if kind == "value1":
                        last = copy(v1_hi[:, 2 * m:2 * m + 2],
                                    out.rearrange("p (j n) -> p j n", j=2)[:, :, 0:C])
                    if kind == "value0":
                        last = copy(v0_hi[:, 4 * m:4 * m + 4], out.rearrange("p (j n) -> p j n", j=4))
                    if kind == "qk":
                        cols = slice(m * HALF, (m + 1) * HALF)
                        activation(q4[0:64, cols], out[0:64, 0:HALF], ACT.Identity, bias=bqk_s[0:64])
                        activation(k4[0:32, cols], out[64:96, 0:HALF], ACT.Identity, bias=bqk_s[64:96])
                        last = activation(k4[96:128, cols], out[96:128, 0:HALF], ACT.Identity, bias=bqk_s[96:128])
                    last.then_inc(S["proj_hi"], 1)

            run_steps(act, c, step)

        @block.vector
        def _(dve):
            c = Counts()
            V = nc.vector

            def link(ins):
                ins.then_inc(S["link"], 1)
                dve.wait_ge(S["link"], c.up("link"))

            def split(hi, lo, src, scale=1.0):
                link(V.tensor_scalar(hi, src, scale, None, ALU.mult))
                return V.scalar_tensor_tensor(lo, src, scale, hi.bitcast(F32), ALU.mult, ALU.subtract)

            dve.wait_ge(loaded0, 16 * 8)
            V.tensor_scalar(gbv[:], bv0_s[:], gamma_s[:], None, ALU.mult).then_inc(bias_ready, 1)
            split(wqk_hi[:], wqk_lo[:], wqk_f)
            split(wv0_hi[:], wv0_lo[:], wv0_f).then_inc(wset0, 1)
            scale = C ** -0.5
            dve.wait_ge(weights_ps, 1)
            split(wqq_hi[:], wqq_lo[:], wqq_ps, scale)
            split(wpv_hi[:, :, 0:C], wpv_lo[:, :, 0:C], wpv_ps)
            for j in range(2):
                split(wpv_hi[:, :, C + j], wpv_lo[:, :, C + j], rowk_ps, scale)
            V.tensor_scalar(query_b[:], query_b_ps, scale, None, ALU.mult)
            dve.wait_ge(ones_ready, 3)
            for cols, by in ((slice(0, C), 1.0), (slice(C, VW), scale)):
                split(value_bh[:, cols], value_b[32:33, cols], value_b_ps[:, cols], by)
            last = V.tensor_copy(value_b[0:1], value_bh[:])
            last.then_inc(weights_ready, 1)
            dve.wait_ge(weights_ready, 1)

            def project_lo(kind, m, slot):
                c.up("proj_hi")
                dve.wait_ge(S["proj_hi"], c.now("proj_hi"))
                out = ring[:, slot]
                if kind == "query":
                    last = V.scalar_tensor_tensor(query_lo[:, m], out, query_b[:, m:m + 1],
                                                  query_hi[:, m].bitcast(F32), ALU.add, ALU.subtract)
                if kind == "value1":
                    out = out.rearrange("p (j n) -> p j n", j=2)
                    two = slice(2 * m, 2 * m + 2)
                    V.tensor_copy(row_const[:, two], out[:, :, C])
                    last = V.tensor_tensor(v1_lo[:, two], out[:, :, 0:C], v1_hi[:, two].bitcast(F32), ALU.subtract)
                if kind == "value0":
                    four = slice(4 * m, 4 * m + 4)
                    last = V.tensor_tensor(v0_lo[:, four], out.rearrange("p (j n) -> p j n", j=4),
                                           v0_hi[:, four].bitcast(F32), ALU.subtract)
                if kind == "qk":
                    cols = slice(m * HALF, (m + 1) * HALF)
                    V.scalar_tensor_tensor(q4[64:128, cols], out[0:64, 0:HALF], bqk_s[0:64],
                                           q4[0:64, cols].bitcast(F32), ALU.add, ALU.subtract)
                    V.scalar_tensor_tensor(k4[32:64, cols], out[64:96, 0:HALF], bk0_s[:],
                                           k4[0:32, cols].bitcast(F32), ALU.add, ALU.subtract)
                    last = V.scalar_tensor_tensor(k4[64:96, cols], out[96:128, 0:HALF], bqk_s[96:128],
                                                  k4[96:128, cols].bitcast(F32), ALU.add, ALU.subtract)
                last.then_inc(S[f"{kind}_split"], 1)

            def norm(m, slot):
                dve.wait_ge(S["ring_ready"], c.now("ring_ready"))
                got = ring[:, slot, 0:CT]
                if m == 0:
                    V.tensor_copy(group_mean[:], got)
                    link(V.tensor_tensor(dev[:], mean_var[:, :, 0], got, ALU.subtract))
                    link(V.tensor_tensor(dev2[:], dev[:], dev[:], ALU.mult))
                    last = V.tensor_tensor(spread[:], dev2[:], mean_var[:, :, 1], ALU.add)
                else:
                    last = V.tensor_scalar(var_eps[:], got, EPS, None, ALU.add)
                last.then_inc(S["norm_read"], 1)

            def add_values(layer, half, ct):
                cols = slice(half * HALF, (half + 1) * HALF)
                dve.wait_ge(S["pv_ready"], c.up("pv_ready"))
                if layer == 0:
                    if half == 0 and ct == 0:
                        dve.wait_ge(S["res0_ready"], c.up("res0_ready"))
                    V.scalar_tensor_tensor(x1[:, ct, cols], pv_ps[:, ct], gamma_s[:], x1[:, ct, cols],
                                           ALU.mult, ALU.add).then_inc(S["pv_read"], 1)
                    dve.wait_ge(S["pv_read"], c.up("pv_read"))
                    link(V.bn_stats(bn[:, ct, half * 6:(half + 1) * 6], x1[:, ct, cols]))
                    if half == HALVES - 1 and ct == CT - 1:
                        dve.sem_inc(dve_passed, 1)
                        V.bn_aggr(mean_var[:, 0], bn[:, 0])
                        V.bn_aggr(mean_var[:, 1], bn[:, 1]).then_inc(S["stats_ready"], 1)
                else:
                    if half == 0 and ct == 0:
                        dve.wait_ge(S["res1_ready"], c.up("res1_ready"))
                    V.tensor_tensor(res1[:, ct, cols], pv_ps[:, ct], res1[:, ct, cols],
                                    ALU.add).then_inc(S["pv_read"], 1)
                    c.up("pv_read")

            def step(has, s):
                if now := tile_before(has, s, 0):
                    layer, k = now
                    bias = neg_max[:, k % 2:k % 2 + 1]
                    dve.wait_ge(S["ring_ready"], c.up("ring_ready"))
                    src = ring[:, AT["tile", s] % 2]
                    if layer == 0:
                        last = V.tensor_reduce(bias, src, AX_X, ALU.max, negate=True)
                    else:
                        link(V.tensor_reduce(neg_raw[:, k % 2:k % 2 + 1], src, AX_X, ALU.max, negate=True))
                        last = V.tensor_scalar(bias, neg_raw[:, k % 2:k % 2 + 1], row_const[:, k:k + 1],
                                               row_const[:, k:k + 1], ALU.subtract, ALU.add)
                    last.then_inc(S["row_ready"], 1)
                last = tile_before(has, s, 1)
                if last:
                    k = last[1] % 2
                    dve.wait_ge(S["exp_done"], c.up("exp_done"))
                    link(V.reciprocal(row_inv[:, k:k + 1], row_sum[:, k:k + 1]))
                if last and last[0] == 0:
                    V.tensor_scalar(prob[:, k], prob[:, k], row_inv[:, k:k + 1], None,
                                    ALU.mult).then_inc(S["p_ready"], 1)
                old = tile_before(has, s, 2)
                if old and old[0] == 0:
                    half, cols = block_of(old[1])
                    dve.wait_ge(S["t_hi"], c.up("t_hi"))
                    V.tensor_tensor(pt_lo[half][:, :, cols], pt_ps[:], pt_hi[half][:, :, cols].bitcast(F32),
                                    ALU.subtract).then_inc(S["t_lo"], 1)
                for kind, m, slot in items(has, s):
                    c.up("ring_ready")
                    if kind == "norm":
                        norm(m, slot)
                    else:
                        project_lo(kind, m, slot)
                part = eighth(has, s)
                if part and part[0] == 0 and part[2] % 2:
                    add_values(0, part[1], part[2] // 2)
                if part and part[0] == 1 and part[2] == 3:
                    for ct in range(CT):
                        add_values(1, part[1], ct)
                if last and last[0] == 1:
                    src = prob[:, k].rearrange("p (m n) -> p m n", n=P)
                    half, cols = block_of(last[1])
                    hi, lo = pt_hi[half][:, :, cols], pt_lo[half][:, :, cols]
                    link(V.tensor_scalar(hi, src, row_inv[:, k:k + 1], None, ALU.mult))
                    V.scalar_tensor_tensor(lo, src, row_inv[:, k:k + 1], hi.bitcast(F32), ALU.mult,
                                           ALU.subtract).then_inc(S["p_split"], 1)

            run_steps(dve, c, step)


def kernel(x, L0_conv_Wq, L0_conv_bq, L0_conv_Wk, L0_conv_bk, L0_conv_Wv, L0_conv_bv, L0_conv_gamma,
           L1_conv_norm_w, L1_conv_norm_b, L1_conv_q_w, L1_conv_q_b, L1_conv_k_w, L1_conv_k_b,
           L1_conv_v_w, L1_conv_v_b, L1_conv_proj_w, L1_conv_proj_b):
    import numpy as np
    import concourse.bacc as bacc
    from concourse.bass_utils import run_bass_kernel_spmd

    def plain(a):
        return np.ascontiguousarray(np.asarray(a))

    def column(b):
        return plain(np.asarray(b).reshape(-1, P).T)

    q, k = np.asarray(L0_conv_Wq), np.asarray(L0_conv_Wk)
    qb, kb = np.asarray(L0_conv_bq), np.asarray(L0_conv_bk)
    arrays = dict(
        x=plain(x).reshape(IMAGES, C, N),
        wqk_t=plain(np.concatenate([q, q, k, k]).T), bqk=plain(np.concatenate([qb, qb, kb, kb])[:, None]),
        bk0=plain(kb[:, None]), wv0_t=plain(np.asarray(L0_conv_Wv).T), bv0=column(L0_conv_bv),
        gamma=plain(np.broadcast_to(np.asarray(L0_conv_gamma), (P, 1))),
        norm_w=column(L1_conv_norm_w), norm_b=column(L1_conv_norm_b),
        wq=plain(L1_conv_q_w), bq=column(L1_conv_q_b), wk=plain(L1_conv_k_w), bk=column(L1_conv_k_b),
        wv=plain(L1_conv_v_w), bv=column(L1_conv_v_b), wp_t=plain(np.asarray(L1_conv_proj_w).T),
        bp=column(L1_conv_proj_b),
        ident=np.eye(P, dtype=np.float32),
        group=np.kron(np.eye(P // GROUP), np.full((GROUP, GROUP), 1 / GROUP)).astype(np.float32),
    )
    nc = bacc.Bacc("TRN2", target_bir_lowering=False, num_devices=1)
    args = {name: nc.dram_tensor(f"in_{name}", a.shape, mybir.dt.from_np(a.dtype), kind="ExternalInput").ap()
            for name, a in arrays.items()}
    args["y"] = nc.dram_tensor("out_y", (IMAGES, C, N), F32, kind="ExternalOutput").ap()
    build(nc, **args)
    run = run_bass_kernel_spmd(nc, [{f"in_{name}": a for name, a in arrays.items()}], core_ids=[0])
    return run.results[0]["out_y"].reshape(np.asarray(x).shape)
```

```python
from contextlib import ExitStack

import concourse.bass as bass
from concourse import mybir
from concourse.alu_op_type import AluOpType as ALU

F32 = mybir.dt.float32
F32R = mybir.dt.float32r
ACT = mybir.ActivationFunctionType
AX_X = mybir.AxisListType.X

IMAGES, C, N = 8, 256, 1024
P = 128
CT = C // P
TILES = N // P
HALF = 512
HALVES = N // HALF
PER_HALF = HALF // P
STEPS = 2 * TILES
PV_LAG = 6
GROUP = 8
EPS = 1e-5
QK = 32
VW = C + 2

ITEMS = {
    0: [("value0", 0)], 1: [("value0", 1)], 2: [("value0", 2)], 3: [("value0", 3)],
    4: [("query", 0)], 5: [("query", 1)],
    6: [("value1", 0)], 7: [("value1", 1)], 8: [("value1", 2)], 9: [("value1", 3)],
    11: [("qk", 0)], 12: [("qk", 1)],
    14: [("norm", 0)], 15: [("norm", 1)],
}
IMAGE_OF = {"query": -1, "value1": -1, "qk": 1, "value0": 0, "norm": 0}
AT = {}
for _s in range(STEPS):
    for _x in [("tile", _s)] + ITEMS.get(_s, []):
        AT[_x] = len(AT)
assert len(AT) % 2 == 0

HEAD = [(-1, s) for s in range(11, STEPS)] + [(0, s) for s in range(STEPS)] + [(1, s) for s in range(PV_LAG)]
TURNS = IMAGES - 2
TAIL = ([(IMAGES - 1, s) for s in range(PV_LAG, STEPS)] + [(IMAGES, s) for s in range(STEPS)]
        + [(IMAGES + 1, s) for s in range(PV_LAG)])
BODY = list(range(PV_LAG, STEPS)) + list(range(PV_LAG))

PER_TURN = dict(
    ring_ready=len(AT), row_ready=16, exp_done=16, inv_ready=16, p_ready=8, p_hi=8, p_split=8, t_ready=8, t_hi=8, t_lo=8,
    pv_ready=8, pv_read=8, qk_split=2, query_split=2, value0_split=4, value1_split=4,
    norm_read=2, block0_free=1, proj_hi=12, stats_ready=1, coef_ready=1, h_hi=2, h_split=1, x_hi=1, x_split=1, res0_ready=1, res1_ready=1,
    link=14)


class Counts:

    def __init__(self):
        self.n = {name: 0 for name in PER_TURN}
        self.turn = None
        self.marks = {}

    def mark(self, place, name):
        self.marks[place] = (name, self.n[name])

    def up(self, name):
        self.n[name] += 1
        return self.now(name)

    def now(self, name):
        return self.at(name, self.n[name])

    def at(self, name, n):
        return n if self.turn is None else n + self.turn * PER_TURN[name]

    def enter(self, turn):
        self.turn, self.before = turn, dict(self.n)

    def leave(self):
        self.marks = {place: (name, n + (TURNS - 1) * PER_TURN[name] if n > self.before[name] else n)
                      for place, (name, n) in self.marks.items()}
        for name, n in self.n.items():
            if n != self.before[name]:
                assert n - self.before[name] == PER_TURN[name], (name, n - self.before[name])
                self.n[name] += (TURNS - 1) * PER_TURN[name]
        self.turn = None


def tile_before(has, s, back):
    i, t = (0, s - back) if s >= back else (-1, s - back + STEPS)
    layer = t // TILES
    return (layer, t % TILES) if has(i - layer) else None


def eighth(has, s):
    i, t = (0, s - PV_LAG) if s >= PV_LAG else (-1, s - PV_LAG + STEPS)
    layer = t // TILES
    return (layer, t % TILES // 4, t % 4) if has(i - layer) else None


def items(has, s):
    return [(kind, m, AT[kind, m] % 2) for kind, m in ITEMS.get(s, []) if has(IMAGE_OF[kind])]


def run_steps(engine, counts, step):
    for i, s in HEAD:
        step(lambda d: 0 <= i + d < IMAGES, s)
    with engine.Fori(0, TURNS) as turn:
        counts.enter(turn)
        for s in BODY:
            step(lambda d: True, s)
        counts.leave()
    for i, s in TAIL:
        step(lambda d: 0 <= i + d < IMAGES, s)


def build(nc, x, wqk_t, bqk, bk0, wv0_t, bv0, gamma, norm_w, norm_b, wq, bq, wk, bk, wv, bv, wp_t, bp,
          ident, group, y):
    with ExitStack() as ctx:
        def sb(name, shape, dt=F32):
            return ctx.enter_context(nc.sbuf_tensor(name, shape, dt))

        def pair(name, shape):
            return sb(name + "_hi", shape, F32R), sb(name + "_lo", shape, F32R)

        def sem(name):
            return ctx.enter_context(nc.semaphore(name))

        x_in = sb("x_in", [P, CT, N])
        x_hi, x_lo = pair("x", [P, CT, N])
        x1 = sb("x1", [P, CT, N])
        h_f = sb("h_f", [P, 2, HALF])
        h_hi, h_lo = pair("h", [P, CT, N])
        res1 = sb("res1", [P, CT, N])
        query_hi, query_lo = pair("query", [P, CT, N])
        v0_hi, v0_lo = pair("v0", [P, TILES, C])
        v1_hi, v1_lo = pair("v1", [P, TILES, C])
        q4 = sb("q4", [P, N], F32R)
        k4 = sb("k4", [P, N], F32R)
        prob = sb("prob", [P, 2, N])
        pt_hi = [sb(f"pt_hi{j}", [P, TILES, HALF], F32R) for j in range(HALVES)]
        pt_lo = [sb(f"pt_lo{j}", [P, TILES, HALF], F32R) for j in range(HALVES)]
        neg_max = sb("neg_max", [P, 2])
        neg_raw = sb("neg_raw", [P, 2])
        row_sum = sb("row_sum", [P, 2])
        row_inv = sb("row_inv", [P, 2])
        row_const = sb("row_const", [P, TILES])
        bn = sb("bn", [P, CT, HALVES * 6])
        mean_var = sb("mean_var", [P, CT, 2])
        group_mean = sb("group_mean", [P, CT])
        dev = sb("dev", [P, CT])
        dev2 = sb("dev2", [P, CT])
        spread = sb("spread", [P, CT])
        var_eps = sb("var_eps", [P, CT])
        rstd = sb("rstd", [P, CT])
        norm_a = sb("norm_a", [P, CT])
        norm_t = sb("norm_t", [P, CT])
        norm_c = sb("norm_c", [P, CT])
        neg_half = sb("neg_half", [P, CT])
        unit = sb("unit", [P, 1])
        wq_f, wk_f, wv_f, wp_f = (prob[:, j // 2, (j % 2) * HALF:(j % 2 + 1) * HALF]
                                  .rearrange("p (t c) -> p t c", t=CT) for j in range(4))
        wqk_f = h_f[:, 0, 0:CT * P].rearrange("p (t c) -> p t c", t=CT)
        wv0_f = h_f[:, 1, :].rearrange("p (t c) -> p t c", t=CT)
        wqk_hi, wqk_lo = pair("wqk", [P, CT, P])
        wv0_hi, wv0_lo = pair("wv0", [P, CT, C])
        wqq_hi, wqq_lo = pair("wqq", [P, CT, C])
        wpv_hi, wpv_lo = pair("wpv", [P, CT, VW])
        bqk_s, bk0_s, gamma_s = sb("bqk_s", [P, 1]), sb("bk0_s", [QK, 1]), sb("gamma_s", [P, 1])
        bv0_s, nw_s, nb_s = sb("bv0_s", [P, CT]), sb("nw_s", [P, CT]), sb("nb_s", [P, CT])
        bq_s, bk_s, bv_s, bp_s = (sb(f"{n}_s", [P, CT]) for n in ("bq", "bk", "bv", "bp"))
        gbv = sb("gbv", [P, CT])
        query_b = sb("query_b", [P, CT])
        value_b = sb("value_b", [P, VW], F32R)
        value_bh = sb("value_bh", [1, VW], F32R)
        ones = sb("ones", [P, P], F32R)
        ident_s, group_s = sb("ident_s", [P, P]), sb("group_s", [P, P])

        ring = ctx.enter_context(nc.psum_tensor("ring", [P, 2, N], F32))
        pt_ps = ctx.enter_context(nc.psum_tensor("pt_ps", [P, TILES, P], F32))
        pv_ps = ctx.enter_context(nc.psum_tensor("pv_ps", [P, CT, HALF], F32))
        wqq_ps = pt_ps[:, 0:4, :].rearrange("p a b -> p (a b)").rearrange("p (t c) -> p t c", t=CT)
        wpv_ps = pt_ps[:, 4:8, :].rearrange("p a b -> p (a b)").rearrange("p (t c) -> p t c", t=CT)
        rowk_ps, query_b_ps = (pv_ps[:, 0, 2 * j:2 * j + 2] for j in range(2))
        value_b_ps = pv_ps[0:1, 1, 0:VW]

        S = {name: sem(name) for name in PER_TURN}
        loaded0, loaded1, x_loaded, y_stored = (sem(n) for n in ("loaded0", "loaded1", "x_loaded", "y_stored"))
        ones_ready, bias_ready, wset0, weights_ps, weights_ready = (
            sem(n) for n in ("ones_ready", "bias_ready", "wset0", "weights_ps", "weights_ready"))
        pool_link = sem("pool_link")
        pool_passed, dve_passed = sem("pool_passed"), sem("dve_passed")

        def block_of(k):
            return k // PER_HALF, slice(k % PER_HALF * P, (k % PER_HALF + 1) * P)

        block = ctx.enter_context(nc.Block())

        x_v = x.rearrange("b (t p) n -> b p t n", p=P)
        y_v = y.rearrange("b (t p) n -> b p t n", p=P)
        by_tile = lambda w: w.rearrange("(t p) c -> p t c", p=P)

        @block.sync
        def _(sp):
            sp.dma_start(x_in[:], x_v[0]).then_inc(x_loaded, 16)
            for dst, src in ((wqk_f, by_tile(wqk_t)), (wv0_f, by_tile(wv0_t)), (bqk_s[:], bqk), (bk0_s[:], bk0),
                             (gamma_s[:], gamma), (bv0_s[:], bv0), (bq_s[:], bq), (bk_s[:], bk)):
                sp.dma_start(dst, src).then_inc(loaded0, 16)
            for dst, src in ((wq_f, by_tile(wq)), (wk_f, by_tile(wk)), (wv_f, by_tile(wv)), (wp_f, by_tile(wp_t)), (bv_s[:], bv), (bp_s[:], bp),
                             (nw_s[:], norm_w), (nb_s[:], norm_b), (ident_s[:], ident), (group_s[:], group)):
                sp.dma_start(dst, src).then_inc(loaded1, 16)

            def load(i):
                sp.wait_ge(S["res0_ready"], i)
                sp.dma_start(x_in[:], x_v[i]).then_inc(x_loaded, 16)

            def store(b):
                n = b * 8 + 8 if not isinstance(b, int) or b < IMAGES - 1 else b * 8 + 4
                for half in range(HALVES):
                    for ct in range(CT):
                        n = n + 1
                        cols = slice(half * HALF, (half + 1) * HALF)
                        sp.wait_ge(S["pv_read"], n)
                        sp.dma_start(y_v[b][:, ct, cols], res1[:, ct, cols]).then_inc(y_stored, 16)

            load(1)
            with sp.Fori(0, IMAGES - 2) as b:
                load(b + 2)
                store(b)
            store(IMAGES - 2)
            store(IMAGES - 1)
            sp.wait_ge(y_stored, IMAGES * 4 * 16)

        @block.gpsimd
        def _(pool):
            LINKS = 3 + 4
            links = [0, None]

            def wait(semaphore, n):
                pool.wait_ge(semaphore, n)
                if not isinstance(n, int):
                    pool.sem_inc(pool_passed, 1)

            def link(ins):
                links[0] += 1
                ins.then_inc(pool_link, 1)
                wait(pool_link, links[0] if links[1] is None else links[0] + links[1] * LINKS)

            def split_x(i):
                if not isinstance(i, int) or i > 0:
                    wait(S["value0_split"], 4 * i)
                wait(S["x_hi"], i + 1)
                for ct in range(CT):
                    last = nc.gpsimd.tensor_tensor(x_lo[:, ct], x_in[:, ct], x_hi[:, ct].bitcast(F32), ALU.subtract)
                last.then_inc(S["x_split"], 1)

            def normalise(b):
                wait(S["norm_read"], 2 * (b + 1))
                link(nc.gpsimd.tensor_tensor(rstd[:], var_eps[:], neg_half[:], ALU.pow))
                link(nc.gpsimd.tensor_tensor(norm_a[:], rstd[:], nw_s[:], ALU.mult))
                link(nc.gpsimd.tensor_tensor(norm_t[:], group_mean[:], norm_a[:], ALU.mult))
                nc.gpsimd.tensor_tensor(norm_c[:], nb_s[:], norm_t[:], ALU.subtract).then_inc(S["coef_ready"], 1)
                wait(S["coef_ready"], b + 1)
                for n in range(4):
                    ct, cols = n // 2, slice(n % 2 * HALF, (n % 2 + 1) * HALF)
                    link(nc.gpsimd.tensor_scalar(h_f[:, n % 2], x1[:, ct, cols], norm_a[:, ct:ct + 1],
                                                 norm_c[:, ct:ct + 1], ALU.mult, ALU.add))
                    if n % 2 == 0:
                        wait(S["h_hi"], 2 * b + 1 + ct)
                    last = nc.gpsimd.tensor_tensor(h_lo[:, ct, cols], h_f[:, n % 2],
                                                   h_hi[:, ct, cols].bitcast(F32), ALU.subtract)
                last.then_inc(S["h_split"], 1)

            def residual1(b):
                if not isinstance(b, int) or b > 0:
                    wait(y_stored, 64 * b)
                for ct in range(CT):
                    last = nc.gpsimd.tensor_scalar(res1[:, ct], x1[:, ct], unit[:], bp_s[:, ct:ct + 1],
                                                   ALU.mult, ALU.add)
                last.then_inc(S["res1_ready"], 1)
                wait(S["res1_ready"], b + 1)

            def residual0(i):
                for ct in range(CT):
                    last = nc.gpsimd.tensor_scalar(x1[:, ct], x_in[:, ct], unit[:], gbv[:, ct:ct + 1],
                                                   ALU.mult, ALU.add)
                last.then_inc(S["res0_ready"], 1)

            nc.gpsimd.memset(ones[:].bitcast(F32), 1.0).then_inc(ones_ready, 1)
            nc.gpsimd.memset(value_b[:].bitcast(F32), 0.0).then_inc(ones_ready, 1)
            nc.gpsimd.memset(neg_half[:], -0.5).then_inc(ones_ready, 1)
            nc.gpsimd.memset(unit[:], 1.0).then_inc(ones_ready, 1)
            wait(ones_ready, 4)
            split_x(0)
            wait(bias_ready, 1)
            residual0(0)
            split_x(1)
            wait(weights_ready, 1)
            with pool.Fori(0, IMAGES - 2) as b:
                links[1] = b
                normalise(b)
                residual1(b)
                residual0(b + 1)
                split_x(b + 2)
            links[0], links[1] = links[0] + (IMAGES - 3) * LINKS, None
            normalise(IMAGES - 2)
            residual1(IMAGES - 2)
            residual0(IMAGES - 1)
            normalise(IMAGES - 1)
            residual1(IMAGES - 1)

        @block.tensor
        def _(pe):
            c = Counts()
            mm = nc.tensor.matmul

            def wait(name, n):
                pe.wait_ge(S[name], c.at(name, n))

            pe.wait_ge(loaded1, 16 * 10)
            pe.wait_ge(loaded0, 16 * 8)
            for ct in range(CT):
                rows = slice(ct * P, (ct + 1) * P)
                for o in range(CT):
                    mm(wqq_ps[:, ct], wq_f[:, o, rows], wk_f[:, o], start=o == 0, stop=o == CT - 1)
                for o in range(CT):
                    mm(wpv_ps[:, ct], wv_f[:, o, rows], wp_f[:, o], start=o == 0, stop=o == CT - 1)
                for out, w, b in ((rowk_ps, wq_f, bk_s), (query_b_ps, wk_f, bq_s)):
                    for o in range(CT):
                        mm(out[:, ct:ct + 1], w[:, o, rows], b[:, o:o + 1], start=o == 0, stop=o == CT - 1)
            for o in range(CT):
                mm(value_b_ps[:, 0:C], bv_s[:, o:o + 1], wp_f[:, o], start=o == 0, stop=o == CT - 1)
            for j in range(2):
                for o in range(CT):
                    last = mm(value_b_ps[:, C + j:C + j + 1], bq_s[:, o:o + 1], bk_s[:, o:o + 1],
                              start=o == 0, stop=o == CT - 1)
            last.then_inc(weights_ps, 1)
            pe.wait_ge(wset0, 1)

            def three(out, w_hi, w_lo, m_hi, m_lo, first, last):
                mm(out, w_hi, m_hi, start=first, stop=False)
                mm(out, w_hi, m_lo, start=False, stop=False)
                return mm(out, w_lo, m_hi, start=False, stop=last)

            def take(*place):
                if place in c.marks:
                    wait(*c.marks[place])

            def logits(layer, k, slot):
                take("slot", slot)
                rows = slice(k * P, (k + 1) * P)
                if k == 0:
                    name = ("qk_split", "query_split")[layer]
                    wait(name, c.n[name])
                for half in range(HALVES):
                    out = ring[:, slot, half * HALF:(half + 1) * HALF]
                    cols = slice(half * HALF, (half + 1) * HALF)
                    if layer == 0:
                        last = mm(out, q4[:, rows], k4[:, cols], start=True, stop=True)
                    else:
                        for ct in range(CT):
                            last = three(out, query_hi[:, ct, rows], query_lo[:, ct, rows],
                                         h_hi[:, ct, cols], h_lo[:, ct, cols], ct == 0, ct == CT - 1)
                last.then_inc(S["ring_ready"], 1)
                c.up("exp_done")
                c.mark(("slot", slot), "exp_done")

            def transposes(k):
                wait("p_ready", c.n["p_ready"] + 1)
                c.up("p_ready")
                if c.n["t_lo"] or c.turn is not None:
                    wait("t_lo", c.n["t_lo"])
                else:
                    pe.wait_ge(weights_ready, 1)
                for st in range(TILES):
                    last = nc.tensor.transpose(pt_ps[:, st], prob[:, k % 2, st * P:(st + 1) * P], ident_s[:])
                last.then_inc(S["t_ready"], 1)
                c.up("t_lo")

            def values0(half, r, tiles):
                ct = r // 2
                if r == 0:
                    wait("value0_split", c.n["value0_split"])
                    wait("t_lo", tiles)
                if r % 2 == 0:
                    take("bank", ct)
                w = slice(ct * P, (ct + 1) * P)
                for st in range(4 * (r % 2), 4 * (r % 2) + 4):
                    last = three(pv_ps[:, ct], v0_hi[:, st, w], v0_lo[:, st, w], pt_hi[half][:, st],
                                 pt_lo[half][:, st], st == 0, st == TILES - 1)
                if r % 2:
                    last.then_inc(S["pv_ready"], 1)
                    c.up("pv_read")
                    c.mark(("bank", ct), "pv_read")

            def values1(half, r):
                if half == 0:
                    if r == 0:
                        wait("value1_split", c.n["value1_split"])
                    c.up("p_split"), c.up("p_split")
                    wait("p_split", c.n["p_split"])
                keys = slice(half * PER_HALF, (half + 1) * PER_HALF)
                two = ((0, 2 * r), (1, 2 * r), (0, 2 * r + 1), (1, 2 * r + 1))
                if r == 3:
                    two = two[0::2] + two[1::2]
                for ct, k in two:
                    if k == 0:
                        take("bank", ct)
                    w = slice(ct * P, (ct + 1) * P)
                    j, cols = block_of(k)
                    last = three(pv_ps[:, ct], v1_hi[:, k, w], v1_lo[:, k, w], pt_hi[j][:, keys, cols],
                                 pt_lo[j][:, keys, cols], k == 0, k == TILES - 1)
                    if half == 1 and (ct, k) == (CT - 1, 0):
                        last.then_inc(S["block0_free"], 1)
                    if k == TILES - 1:
                        last.then_inc(S["pv_ready"], 1)
                        c.up("pv_read")
                        c.mark(("bank", ct), "pv_read")

            def project(kind, m, slot):
                out = ring[:, slot]
                reader = {"norm": "norm_read"}.get(kind, f"{kind}_split")
                if kind == "query":
                    if m == 0:
                        pe.wait_ge(S["h_split"], c.up("h_split"))
                    take("slot", slot)
                    for half in range(HALVES):
                        cols = slice(half * HALF, (half + 1) * HALF)
                        for ct in range(CT):
                            w = (slice(None), ct, slice(m * P, (m + 1) * P))
                            last = three(out[:, cols], wqq_hi[w], wqq_lo[w], h_hi[:, ct, cols],
                                         h_lo[:, ct, cols], ct == 0, ct == CT - 1)
                if kind == "value1":
                    take("slot", slot)
                    for j in range(2):
                        mm(out[:, j * HALF:j * HALF + VW], ones[:], value_b[:], start=True, stop=False)
                        for ct in range(CT):
                            w = (slice(None), ct, slice((2 * m + j) * P, (2 * m + j + 1) * P))
                            last = three(out[:, j * HALF:j * HALF + VW], h_hi[w], h_lo[w], wpv_hi[:, ct],
                                         wpv_lo[:, ct], False, ct == CT - 1)
                if kind == "qk":
                    if m == 0:
                        pe.wait_ge(S["x_split"], c.up("x_split"))
                    take("slot", slot)
                    cols = slice(m * HALF, (m + 1) * HALF)
                    for ct in range(CT):
                        last = three(out[:, 0:HALF], wqk_hi[:, ct], wqk_lo[:, ct], x_hi[:, ct, cols],
                                     x_lo[:, ct, cols], ct == 0, ct == CT - 1)
                if kind == "value0":
                    take("slot", slot)
                    for j in range(2):
                        for ct in range(CT):
                            w = (slice(None), ct, slice((2 * m + j) * P, (2 * m + j + 1) * P))
                            last = three(out[:, j * C:(j + 1) * C], x_hi[w], x_lo[w], wv0_hi[:, ct],
                                         wv0_lo[:, ct], ct == 0, ct == CT - 1)
                if kind == "norm":
                    if m == 0:
                        pe.wait_ge(S["stats_ready"], c.up("stats_ready"))
                    else:
                        wait("norm_read", c.n["norm_read"])
                    take("slot", slot)
                    last = mm(out[:, 0:CT], group_s[:], mean_var[:, :, 0] if m == 0 else spread[:],
                              start=True, stop=True)
                last.then_inc(S["ring_ready"], 1)
                c.up(reader)
                c.mark(("slot", slot), reader)

            def step(has, s):
                if now := tile_before(has, s, 0):
                    logits(*now, AT["tile", s] % 2)
                late = [item for item in items(has, s) if s == 2 or item[:2] == ("norm", 0)]
                for item in items(has, s):
                    if item not in late:
                        project(*item)
                if part := eighth(has, s):
                    layer, half, r = part
                    if layer == 0:
                        old = tile_before(has, s, 2)
                        values0(half, r, c.n["t_lo"] - bool(old and old[0] == 0))
                    else:
                        values1(half, r)
                for item in late:
                    project(*item)
                if (old := tile_before(has, s, 1)) and old[0] == 0:
                    transposes(old[1])

            run_steps(pe, c, step)

        @block.scalar
        def _(act):
            c = Counts()
            copy, activation = nc.scalar.copy, nc.scalar.activation

            def x_to_hi():
                act.wait_ge(x_loaded, 16 * c.up("x_hi"))
                for ct in range(CT):
                    last = copy(x_hi[:, ct], x_in[:, ct])
                last.then_inc(S["x_hi"], 1)

            def rows_hi(k, inverse):
                half, cols = block_of(k)
                if k % PER_HALF == 0:
                    act.wait_ge(S["pv_ready"], c.now("pv_ready"))
                act.wait_ge(S["inv_ready"], inverse)
                activation(pt_hi[half][:, :, cols], prob[:, k % 2].rearrange("p (m n) -> p m n", n=P),
                           ACT.Identity, scale=row_inv[:, k % 2:k % 2 + 1]).then_inc(S["p_hi"], 1)

            def step(has, s):
                old = tile_before(has, s, 2)
                if previous := tile_before(has, s, 1):
                    inverse = c.up("inv_ready")
                if previous and previous[0] == 1 and previous[1] % PER_HALF:
                    rows_hi(previous[1], inverse)
                if old and old[0] == 0:
                    half, cols = block_of(old[1])
                    if old[1] == 0 and has(-2):
                        act.wait_ge(S["block0_free"], c.up("block0_free"))
                    act.wait_ge(S["t_ready"], c.up("t_ready"))
                    copy(pt_hi[half][:, :, cols], pt_ps[:]).then_inc(S["t_hi"], 1)
                if now := tile_before(has, s, 0):
                    k, slot = now[1], AT["tile", s] % 2
                    act.wait_ge(S["row_ready"], c.up("row_ready"))
                    activation(prob[:, k % 2], ring[:, slot], ACT.Exp, bias=neg_max[:, k % 2:k % 2 + 1],
                               accum_out=row_sum[:, k % 2:k % 2 + 1]).then_inc(S["exp_done"], 1)
                    c.up("ring_ready")
                for kind, m, slot in items(has, s):
                    ready = c.up("ring_ready")
                    if kind == "norm":
                        continue
                    act.wait_ge(S["ring_ready"], ready)
                    out = ring[:, slot]
                    if kind == "query":
                        last = activation(query_hi[:, m], out, ACT.Identity, bias=query_b[:, m:m + 1])
                    if kind == "value1":
                        last = copy(v1_hi[:, 2 * m:2 * m + 2],
                                    out.rearrange("p (j n) -> p j n", j=2)[:, :, 0:C])
                    if kind == "value0":
                        last = copy(v0_hi[:, 2 * m:2 * m + 2],
                                    out[:, 0:HALF].rearrange("p (j n) -> p j n", j=2))
                    if kind == "qk":
                        cols = slice(m * HALF, (m + 1) * HALF)
                        activation(q4[0:64, cols], out[0:64, 0:HALF], ACT.Identity, bias=bqk_s[0:64])
                        activation(k4[0:32, cols], out[64:96, 0:HALF], ACT.Identity, bias=bqk_s[64:96])
                        last = activation(k4[96:128, cols], out[96:128, 0:HALF], ACT.Identity, bias=bqk_s[96:128])
                    last.then_inc(S["proj_hi"], 1)
                if s in (0, 1) and has(-1):
                    if s == 0:
                        act.wait_ge(S["coef_ready"], c.up("coef_ready"))
                    activation(h_hi[:, s], x1[:, s], ACT.Identity, bias=norm_c[:, s:s + 1],
                               scale=norm_a[:, s:s + 1]).then_inc(S["h_hi"], 1)
                if s == 8 and has(1):
                    x_to_hi()
                part = eighth(has, s)
                if part and part[0] == 0 and part[2] % 2:
                    c.up("pv_ready")
                if part and part[0] == 1 and part[2] == 3:
                    c.up("pv_ready"), c.up("pv_ready")
                if previous and previous[0] == 1 and previous[1] % PER_HALF == 0:
                    rows_hi(previous[1], inverse)

            x_to_hi()
            run_steps(act, c, step)

        @block.vector
        def _(dve):
            c = Counts()
            V = nc.vector

            def link(ins):
                ins.then_inc(S["link"], 1)
                dve.wait_ge(S["link"], c.up("link"))

            def split(hi, lo, src, scale=1.0):
                link(V.tensor_scalar(hi, src, scale, None, ALU.mult))
                return V.scalar_tensor_tensor(lo, src, scale, hi.bitcast(F32), ALU.mult, ALU.subtract)

            dve.wait_ge(loaded0, 16 * 8)
            V.tensor_scalar(gbv[:], bv0_s[:], gamma_s[:], None, ALU.mult).then_inc(bias_ready, 1)
            split(wqk_hi[:], wqk_lo[:], wqk_f)
            split(wv0_hi[:], wv0_lo[:], wv0_f).then_inc(wset0, 1)
            scale = C ** -0.5
            dve.wait_ge(weights_ps, 1)
            split(wqq_hi[:], wqq_lo[:], wqq_ps, scale)
            split(wpv_hi[:, :, 0:C], wpv_lo[:, :, 0:C], wpv_ps)
            for j in range(2):
                split(wpv_hi[:, :, C + j], wpv_lo[:, :, C + j], rowk_ps, scale)
            V.tensor_scalar(query_b[:], query_b_ps, scale, None, ALU.mult)
            dve.wait_ge(ones_ready, 4)
            for cols, by in ((slice(0, C), 1.0), (slice(C, VW), scale)):
                split(value_bh[:, cols], value_b[32:33, cols], value_b_ps[:, cols], by)
            last = V.tensor_copy(value_b[0:1], value_bh[:])
            last.then_inc(weights_ready, 1)
            dve.wait_ge(weights_ready, 1)

            def project_lo(kind, m, slot):
                c.up("proj_hi")
                dve.wait_ge(S["proj_hi"], c.now("proj_hi"))
                out = ring[:, slot]
                if kind == "query":
                    last = V.scalar_tensor_tensor(query_lo[:, m], out, query_b[:, m:m + 1],
                                                  query_hi[:, m].bitcast(F32), ALU.add, ALU.subtract)
                if kind == "value1":
                    out = out.rearrange("p (j n) -> p j n", j=2)
                    two = slice(2 * m, 2 * m + 2)
                    V.tensor_copy(row_const[:, two], out[:, :, C])
                    last = V.tensor_tensor(v1_lo[:, two], out[:, :, 0:C], v1_hi[:, two].bitcast(F32), ALU.subtract)
                if kind == "value0":
                    two = slice(2 * m, 2 * m + 2)
                    last = V.tensor_tensor(v0_lo[:, two], out[:, 0:HALF].rearrange("p (j n) -> p j n", j=2),
                                           v0_hi[:, two].bitcast(F32), ALU.subtract)
                if kind == "qk":
                    cols = slice(m * HALF, (m + 1) * HALF)
                    V.scalar_tensor_tensor(q4[64:128, cols], out[0:64, 0:HALF], bqk_s[0:64],
                                           q4[0:64, cols].bitcast(F32), ALU.add, ALU.subtract)
                    V.scalar_tensor_tensor(k4[32:64, cols], out[64:96, 0:HALF], bk0_s[:],
                                           k4[0:32, cols].bitcast(F32), ALU.add, ALU.subtract)
                    last = V.scalar_tensor_tensor(k4[64:96, cols], out[96:128, 0:HALF], bqk_s[96:128],
                                                  k4[96:128, cols].bitcast(F32), ALU.add, ALU.subtract)
                last.then_inc(S[f"{kind}_split"], 1)

            def norm(m, slot):
                dve.wait_ge(S["ring_ready"], c.now("ring_ready"))
                got = ring[:, slot, 0:CT]
                if m == 0:
                    V.tensor_copy(group_mean[:], got)
                    link(V.tensor_tensor(dev[:], mean_var[:, :, 0], got, ALU.subtract))
                    link(V.tensor_tensor(dev2[:], dev[:], dev[:], ALU.mult))
                    last = V.tensor_tensor(spread[:], dev2[:], mean_var[:, :, 1], ALU.add)
                else:
                    last = V.tensor_scalar(var_eps[:], got, EPS, None, ALU.add)
                last.then_inc(S["norm_read"], 1)

            def add_values(layer, half, ct):
                cols = slice(half * HALF, (half + 1) * HALF)
                dve.wait_ge(S["pv_ready"], c.up("pv_ready"))
                if layer == 0:
                    if half == 0 and ct == 0:
                        dve.wait_ge(S["res0_ready"], c.up("res0_ready"))
                    V.scalar_tensor_tensor(x1[:, ct, cols], pv_ps[:, ct], gamma_s[:], x1[:, ct, cols],
                                           ALU.mult, ALU.add).then_inc(S["pv_read"], 1)
                    dve.wait_ge(S["pv_read"], c.up("pv_read"))
                    link(V.bn_stats(bn[:, ct, half * 6:(half + 1) * 6], x1[:, ct, cols]))
                    if half == HALVES - 1 and ct == CT - 1:
                        dve.sem_inc(dve_passed, 1)
                        V.bn_aggr(mean_var[:, 0], bn[:, 0])
                        V.bn_aggr(mean_var[:, 1], bn[:, 1]).then_inc(S["stats_ready"], 1)
                else:
                    if half == 0 and ct == 0:
                        dve.wait_ge(S["res1_ready"], c.up("res1_ready"))
                    V.tensor_tensor(res1[:, ct, cols], pv_ps[:, ct], res1[:, ct, cols],
                                    ALU.add).then_inc(S["pv_read"], 1)
                    c.up("pv_read")

            def rows_lo(k):
                src = prob[:, k % 2].rearrange("p (m n) -> p m n", n=P)
                half, cols = block_of(k)
                hi, lo = pt_hi[half][:, :, cols], pt_lo[half][:, :, cols]
                dve.wait_ge(S["p_hi"], c.up("p_hi"))
                V.scalar_tensor_tensor(lo, src, row_inv[:, k % 2:k % 2 + 1], hi.bitcast(F32), ALU.mult,
                                       ALU.subtract).then_inc(S["p_split"], 1)

            def step(has, s):
                if previous := tile_before(has, s, 1):
                    k = previous[1] % 2
                    dve.wait_ge(S["exp_done"], c.up("exp_done"))
                    V.reciprocal(row_inv[:, k:k + 1], row_sum[:, k:k + 1]).then_inc(S["inv_ready"], 1)
                    dve.wait_ge(S["inv_ready"], c.up("inv_ready"))
                    if previous[0] == 0:
                        V.tensor_scalar(prob[:, k], prob[:, k], row_inv[:, k:k + 1], None,
                                        ALU.mult).then_inc(S["p_ready"], 1)
                if now := tile_before(has, s, 0):
                    layer, k = now
                    bias = neg_max[:, k % 2:k % 2 + 1]
                    dve.wait_ge(S["ring_ready"], c.up("ring_ready"))
                    src = ring[:, AT["tile", s] % 2]
                    if layer == 0:
                        max_of = V.tensor_reduce(bias, src, AX_X, ALU.max, negate=True)
                    else:
                        link(V.tensor_reduce(neg_raw[:, k % 2:k % 2 + 1], src, AX_X, ALU.max, negate=True))
                        max_of = V.tensor_scalar(bias, neg_raw[:, k % 2:k % 2 + 1], row_const[:, k:k + 1],
                                                 row_const[:, k:k + 1], ALU.subtract, ALU.add)
                    max_of.then_inc(S["row_ready"], 1)
                old = tile_before(has, s, 2)
                if old and old[0] == 0:
                    half, cols = block_of(old[1])
                    dve.wait_ge(S["t_hi"], c.up("t_hi"))
                    V.tensor_tensor(pt_lo[half][:, :, cols], pt_ps[:], pt_hi[half][:, :, cols].bitcast(F32),
                                    ALU.subtract).then_inc(S["t_lo"], 1)
                if previous and previous[0] == 1 and previous[1] % PER_HALF:
                    rows_lo(previous[1])
                for kind, m, slot in items(has, s):
                    c.up("ring_ready")
                    if kind == "norm":
                        norm(m, slot)
                    else:
                        project_lo(kind, m, slot)
                part = eighth(has, s)
                if part and part[0] == 0 and part[2] % 2:
                    add_values(0, part[1], part[2] // 2)
                if part and part[0] == 1 and part[2] == 3:
                    for ct in range(CT):
                        add_values(1, part[1], ct)
                if previous and previous[0] == 1 and previous[1] % PER_HALF == 0:
                    rows_lo(previous[1])

            run_steps(dve, c, step)


def kernel(x, L0_conv_Wq, L0_conv_bq, L0_conv_Wk, L0_conv_bk, L0_conv_Wv, L0_conv_bv, L0_conv_gamma,
           L1_conv_norm_w, L1_conv_norm_b, L1_conv_q_w, L1_conv_q_b, L1_conv_k_w, L1_conv_k_b,
           L1_conv_v_w, L1_conv_v_b, L1_conv_proj_w, L1_conv_proj_b):
    import numpy as np
    import concourse.bacc as bacc
    from concourse.bass_utils import run_bass_kernel_spmd

    def plain(a):
        return np.ascontiguousarray(np.asarray(a))

    def column(b):
        return plain(np.asarray(b).reshape(-1, P).T)

    q, k = np.asarray(L0_conv_Wq), np.asarray(L0_conv_Wk)
    qb, kb = np.asarray(L0_conv_bq), np.asarray(L0_conv_bk)
    arrays = dict(
        x=plain(x).reshape(IMAGES, C, N),
        wqk_t=plain(np.concatenate([q, q, k, k]).T), bqk=plain(np.concatenate([qb, qb, kb, kb])[:, None]),
        bk0=plain(kb[:, None]), wv0_t=plain(np.asarray(L0_conv_Wv).T), bv0=column(L0_conv_bv),
        gamma=plain(np.broadcast_to(np.asarray(L0_conv_gamma), (P, 1))),
        norm_w=column(L1_conv_norm_w), norm_b=column(L1_conv_norm_b),
        wq=plain(L1_conv_q_w), bq=column(L1_conv_q_b), wk=plain(L1_conv_k_w), bk=column(L1_conv_k_b),
        wv=plain(L1_conv_v_w), bv=column(L1_conv_v_b), wp_t=plain(np.asarray(L1_conv_proj_w).T),
        bp=column(L1_conv_proj_b),
        ident=np.eye(P, dtype=np.float32),
        group=np.kron(np.eye(P // GROUP), np.full((GROUP, GROUP), 1 / GROUP)).astype(np.float32),
    )
    nc = bacc.Bacc("TRN2", target_bir_lowering=False, num_devices=1)
    args = {name: nc.dram_tensor(f"in_{name}", a.shape, mybir.dt.from_np(a.dtype), kind="ExternalInput").ap()
            for name, a in arrays.items()}
    args["y"] = nc.dram_tensor("out_y", (IMAGES, C, N), F32, kind="ExternalOutput").ap()
    build(nc, **args)
    run = run_bass_kernel_spmd(nc, [{f"in_{name}": a for name, a in arrays.items()}], core_ids=[0])
    return run.results[0]["out_y"].reshape(np.asarray(x).shape)
```

```python
from contextlib import ExitStack

import concourse.bass as bass
from concourse import mybir
from concourse.alu_op_type import AluOpType as ALU

F32 = mybir.dt.float32
F32R = mybir.dt.float32r
ACT = mybir.ActivationFunctionType
AX_X = mybir.AxisListType.X

IMAGES, C, N = 8, 256, 1024
P = 128
CT = C // P
TILES = N // P
HALF = 512
HALVES = N // HALF
PER_HALF = HALF // P
STEPS = 2 * TILES
PV_LAG = 6
GROUP = 8
EPS = 1e-5
QK = 32
VW = C + 2

ITEMS = {
    0: [("value0", 0)], 1: [("value0", 1)], 2: [("value0", 2)], 3: [("value0", 3)],
    4: [("query", 0)], 5: [("query", 1)],
    6: [("value1", 0)], 7: [("value1", 1)], 8: [("value1", 2)], 9: [("value1", 3)],
    10: [("qk", 0)], 12: [("qk", 1)],
    14: [("norm", 0)], 15: [("norm", 1)],
}
IMAGE_OF = {"query": -1, "value1": -1, "qk": 1, "value0": 0, "norm": 0}
VALUES_FIRST = TILES + 1 + PER_HALF
RING_USES = STEPS + sum(len(some) for some in ITEMS.values())
assert RING_USES % 2 == 0

PER_TURN = dict(
    ring_ready=RING_USES, row_ready=16, exp_done=16, inv_ready=16,
    p_ready=8, t_ready=8, t_hi=8, t_lo=8,
    p_hi=8, p_split=8, block0_free=1,
    pv_ready=8, pv_read=8,
    proj_hi=8, qk_split=2, query_split=2, value0_split=4,
    v1_full=4, v1_hi=4, value1_split=4,
    stats_ready=1, norm_read=2, coef_ready=1, h_hi=2, h_split=1,
    x_hi=2, x_split=2, res0_ready=1, res1_ready=1,
    link=14, bias_read=0)


class Counts:

    def __init__(self):
        self.n = {name: 0 for name in PER_TURN}
        self.turn = None
        self.marks = {}

    def mark(self, place, name):
        self.marks[place] = (name, self.n[name])

    def up(self, name):
        self.n[name] += 1
        return self.now(name)

    def now(self, name):
        return self.at(name, self.n[name])

    def at(self, name, n):
        return n if self.turn is None else n + self.turn * PER_TURN[name]

    def enter(self, turn):
        self.turn, self.before = turn, dict(self.n)

    def leave(self):
        self.marks = {place: (name, n + (TURNS - 1) * PER_TURN[name] if n > self.before[name] else n)
                      for place, (name, n) in self.marks.items()}
        for name, n in self.n.items():
            if n != self.before[name]:
                assert n - self.before[name] == PER_TURN[name], (name, n - self.before[name])
                self.n[name] += (TURNS - 1) * PER_TURN[name]
        self.turn = None


class Step:

    def __init__(self, tile, items, parts, values_first, h, load_x, block0):
        self.tile = tile
        self.previous = self.old = None
        self.items = list(items)
        self.late = []
        self.parts = list(parts)
        self.values_first = values_first
        self.h = h
        self.load_x = load_x
        self.block0 = block0
        self.hi_first = False
        self.slot = {}

    def entries(self):
        return [("tile",)] * bool(self.tile) + self.items


def regular(has, s):
    def there(layer_tile, turn):
        return layer_tile if has(turn - layer_tile[0]) else None

    def tile(back):
        return there(((s - back) % STEPS // TILES, (s - back) % TILES), 0 if s >= back else -1)

    t = (s - PV_LAG) % STEPS
    part = there((t // TILES, t % TILES // 4, t % 4), 0 if s >= PV_LAG else -1)
    step = Step(tile(0), [(kind, m) for kind, m in ITEMS.get(s, []) if has(IMAGE_OF[kind])],
                [part] if part else [], values_first=s == VALUES_FIRST,
                h=(s,) if s < CT and has(-1) else (), load_x=s == TILES and has(1),
                block0=s == 2 and has(-2))
    step.previous, step.old = tile(1), tile(2)
    step.late = [item for item in step.items if s == 2 or item == ("norm", 0)]
    return step


def take_slots(steps, first):
    n = first
    for step in steps:
        for entry in step.entries():
            step.slot[entry] = n % 2
            n += 1
    return steps


def span(*turns):
    return [regular(lambda d: 0 <= i + d < IMAGES, s) for i, steps in turns for s in steps]


FIRST = 3
HEAD = span((-1, (10, 11, 12)), (0, range(STEPS)), (1, range(PV_LAG)))
HEAD[FIRST + 14].items.insert(0, ("bias", 0))
for _step in HEAD:
    _step.hi_first = True
take_slots(HEAD, 0)

TURNS = IMAGES - 2
LOOP = take_slots([regular(lambda d: True, s) for s in (*range(PV_LAG, STEPS), *range(PV_LAG))], 0)
TAIL = take_slots(span((IMAGES - 1, range(PV_LAG, STEPS)), (IMAGES, range(STEPS)), (IMAGES + 1, range(PV_LAG))), 0)


def run_steps(engine, counts, step, setup={}):
    for n, now in enumerate(HEAD):
        if n in setup:
            setup[n]()
        step(now)
    with engine.Fori(0, TURNS) as turn:
        counts.enter(turn)
        for now in LOOP:
            step(now)
        counts.leave()
    for now in TAIL:
        step(now)


def build(nc, x, wqk_t, bqk, bk0, wv0_t, bv0, gamma, norm_w, norm_b, wq, bq, wk, bk, wv, bv, wp_t, bp,
          ident, group, y):
    with ExitStack() as ctx:
        def sb(name, shape, dt=F32):
            return ctx.enter_context(nc.sbuf_tensor(name, shape, dt))

        def pair(name, shape):
            return sb(name + "_hi", shape, F32R), sb(name + "_lo", shape, F32R)

        def sem(name):
            return ctx.enter_context(nc.semaphore(name))

        x_in = sb("x_in", [P, CT, N])
        x_hi, x_lo = pair("x", [P, CT, N])
        x1 = sb("x1", [P, CT, N])
        h_f = sb("h_f", [P, 2, HALF])
        h_hi, h_lo = pair("h", [P, CT, N])
        res1 = sb("res1", [P, CT, N])
        query_hi, query_lo = pair("query", [P, CT, N])
        v0_hi, v0_lo = pair("v0", [P, TILES, C])
        v1_hi, v1_lo = pair("v1", [P, TILES, C])
        q4 = sb("q4", [P, N], F32R)
        k4 = sb("k4", [P, N], F32R)
        prob = sb("prob", [P, 2, N])
        pt_hi = [sb(f"pt_hi{j}", [P, TILES, HALF], F32R) for j in range(HALVES)]
        pt_lo = [sb(f"pt_lo{j}", [P, TILES, HALF], F32R) for j in range(HALVES)]
        neg_max = sb("neg_max", [P, 2])
        neg_raw = sb("neg_raw", [P, 2])
        row_sum = sb("row_sum", [P, 2])
        row_inv = sb("row_inv", [P, 2])
        row_const = sb("row_const", [P, TILES])
        bn = sb("bn", [P, CT, HALVES * 6])
        mean_var = sb("mean_var", [P, CT, 2])
        group_mean = sb("group_mean", [P, CT])
        dev = sb("dev", [P, CT])
        dev2 = sb("dev2", [P, CT])
        spread = sb("spread", [P, CT])
        var_eps = sb("var_eps", [P, CT])
        rstd = sb("rstd", [P, CT])
        norm_a = sb("norm_a", [P, CT])
        norm_t = sb("norm_t", [P, CT])
        norm_c = sb("norm_c", [P, CT])
        neg_half = sb("neg_half", [P, CT])
        unit = sb("unit", [P, 1])
        wq_f, wk_f, wv_f, wp_f = (res1[:, j // 2, (j % 2) * HALF:(j % 2 + 1) * HALF]
                                  .rearrange("p (t c) -> p t c", t=CT) for j in range(4))
        wqk_f = h_f[:, 0, 0:CT * P].rearrange("p (t c) -> p t c", t=CT)
        wv0_f = h_f[:, 1, :].rearrange("p (t c) -> p t c", t=CT)
        wqk_hi, wqk_lo = pair("wqk", [P, CT, P])
        wv0_hi, wv0_lo = pair("wv0", [P, CT, C])
        wqq_hi, wqq_lo = pair("wqq", [P, CT, C])
        wpv_hi, wpv_lo = pair("wpv", [P, CT, VW])
        bqk_s, bk0_s, gamma_s = sb("bqk_s", [P, 1]), sb("bk0_s", [QK, 1]), sb("gamma_s", [P, 1])
        bv0_s, nw_s, nb_s = sb("bv0_s", [P, CT]), sb("nw_s", [P, CT]), sb("nb_s", [P, CT])
        bq_s, bk_s, bv_s, bp_s = (sb(f"{n}_s", [P, CT]) for n in ("bq", "bk", "bv", "bp"))
        gbv = sb("gbv", [P, CT])
        query_b = sb("query_b", [P, CT])
        value_b = sb("value_b", [P, VW])
        v1_f = h_f[:].rearrange("p s (j c) -> p s j c", j=2)
        bv_rows, bq_rows = sb("bv_rows", [P, CT, P]), sb("bq_rows", [P, CT, P])
        ones = sb("ones", [P, P])
        ident_s, group_s = sb("ident_s", [P, P]), sb("group_s", [P, P])

        ring = ctx.enter_context(nc.psum_tensor("ring", [P, 2, N], F32))
        pt_ps = ctx.enter_context(nc.psum_tensor("pt_ps", [P, TILES, P], F32))
        pv_ps = ctx.enter_context(nc.psum_tensor("pv_ps", [P, CT, HALF], F32))
        wqq_ps, wpv_ps = (pv_ps[:, j].rearrange("p (t c) -> p t c", t=CT) for j in range(2))

        def bias_places(out):
            return out[:, 0:VW], out[:, VW:VW + CT], out[:, VW + CT:VW + 2 * CT]

        S = {name: sem(name) for name in PER_TURN}
        wqk_loaded, wv0_loaded, weights_loaded = (sem(n) for n in ("wqk_loaded", "wv0_loaded", "weights_loaded"))
        x0_loaded = [sem(f"x0_loaded{half}") for half in range(HALVES)]
        x_loaded, y_stored = sem("x_loaded"), sem("y_stored")
        ones_ready, bias_ready, layer0_split, weights_ps, weights_read = (
            sem(n) for n in ("ones_ready", "bias_ready", "layer0_split", "weights_ps", "weights_read"))
        pool_link = sem("pool_link")
        pool_passed, dve_passed = sem("pool_passed"), sem("dve_passed")

        def block_of(k):
            return k // PER_HALF, slice(k % PER_HALF * P, (k % PER_HALF + 1) * P)

        block = ctx.enter_context(nc.Block())

        x_v = x.rearrange("b (t p) n -> b p t n", p=P)
        y_v = y.rearrange("b (t p) n -> b p t n", p=P)
        by_tile = lambda w: w.rearrange("(t p) c -> p t c", p=P)

        @block.sync
        def _(sp):
            halves = [slice(half * HALF, (half + 1) * HALF) for half in range(HALVES)]
            for ready, loads in (
                    (wqk_loaded, ((wqk_f, by_tile(wqk_t)), (bqk_s[:], bqk), (bk0_s[:], bk0))),
                    (x0_loaded[0], ((x_in[:, :, halves[0]], x_v[0][:, :, halves[0]]),)),
                    (x0_loaded[1], ((x_in[:, :, halves[1]], x_v[0][:, :, halves[1]]),)),
                    (wv0_loaded, ((wv0_f, by_tile(wv0_t)), (bv0_s[:], bv0), (gamma_s[:], gamma))),
                    (weights_loaded, ((wq_f, by_tile(wq)), (wk_f, by_tile(wk)), (wv_f, by_tile(wv)),
                                      (wp_f, by_tile(wp_t)), (ident_s[:], ident), (bq_s[:], bq), (bk_s[:], bk),
                                      (bv_s[:], bv), (bp_s[:], bp), (nw_s[:], norm_w), (nb_s[:], norm_b),
                                      (group_s[:], group)))):
                for dst, src in loads:
                    sp.dma_start(dst, src).then_inc(ready, 16)

            def load(i):
                sp.wait_ge(S["res0_ready"], i)
                sp.dma_start(x_in[:], x_v[i]).then_inc(x_loaded, 16)

            def store(b):
                n = b * 8 + 8 if not isinstance(b, int) or b < IMAGES - 1 else b * 8 + 4
                for half in range(HALVES):
                    for ct in range(CT):
                        n = n + 1
                        cols = slice(half * HALF, (half + 1) * HALF)
                        sp.wait_ge(S["pv_read"], n)
                        sp.dma_start(y_v[b][:, ct, cols], res1[:, ct, cols]).then_inc(y_stored, 16)

            load(1)
            with sp.Fori(0, IMAGES - 2) as b:
                load(b + 2)
                store(b)
            store(IMAGES - 2)
            store(IMAGES - 1)
            sp.wait_ge(y_stored, IMAGES * 4 * 16)

        @block.gpsimd
        def _(pool):
            LINKS = 3 + 4
            links = [0, None]

            def wait(semaphore, n):
                pool.wait_ge(semaphore, n)
                if not isinstance(n, int):
                    pool.sem_inc(pool_passed, 1)

            def link(ins):
                links[0] += 1
                ins.then_inc(pool_link, 1)
                wait(pool_link, links[0] if links[1] is None else links[0] + links[1] * LINKS)

            def split_x(i, half):
                if half == 0:
                    wait(S["value0_split"], 4 * i)
                cols = slice(half * HALF, (half + 1) * HALF)
                wait(S["x_hi"], 2 * i + 1 + half)
                nc.gpsimd.tensor_tensor(x_lo[:, :, cols], x_in[:, :, cols], x_hi[:, :, cols].bitcast(F32),
                                        ALU.subtract).then_inc(S["x_split"], 1)

            def split_value1(b, m):
                wait(S["v1_hi"], 4 * b + m + 1)
                two = slice(2 * m, 2 * m + 2)
                nc.gpsimd.tensor_tensor(v1_lo[:, two], v1_f[:, m % 2], v1_hi[:, two].bitcast(F32),
                                        ALU.subtract).then_inc(S["value1_split"], 1)

            def normalise(b):
                wait(S["norm_read"], 2 * (b + 1))
                link(nc.gpsimd.tensor_tensor(rstd[:], var_eps[:], neg_half[:], ALU.pow))
                link(nc.gpsimd.tensor_tensor(norm_a[:], rstd[:], nw_s[:], ALU.mult))
                link(nc.gpsimd.tensor_tensor(norm_t[:], group_mean[:], norm_a[:], ALU.mult))
                nc.gpsimd.tensor_tensor(norm_c[:], nb_s[:], norm_t[:], ALU.subtract).then_inc(S["coef_ready"], 1)
                wait(S["coef_ready"], b + 1)
                for n in range(4):
                    ct, cols = n // 2, slice(n % 2 * HALF, (n % 2 + 1) * HALF)
                    link(nc.gpsimd.tensor_scalar(h_f[:, n % 2], x1[:, ct, cols], norm_a[:, ct:ct + 1],
                                                 norm_c[:, ct:ct + 1], ALU.mult, ALU.add))
                    if n % 2 == 0:
                        wait(S["h_hi"], 2 * b + 1 + ct)
                    last = nc.gpsimd.tensor_tensor(h_lo[:, ct, cols], h_f[:, n % 2],
                                                   h_hi[:, ct, cols].bitcast(F32), ALU.subtract)
                last.then_inc(S["h_split"], 1)

            def residual1(b):
                if not isinstance(b, int) or b > 0:
                    wait(y_stored, 64 * b)
                for ct in range(CT):
                    last = nc.gpsimd.tensor_scalar(res1[:, ct], x1[:, ct], unit[:], bp_s[:, ct:ct + 1],
                                                   ALU.mult, ALU.add)
                last.then_inc(S["res1_ready"], 1)
                wait(S["res1_ready"], b + 1)

            def residual0(i):
                for ct in range(CT):
                    last = nc.gpsimd.tensor_scalar(x1[:, ct], x_in[:, ct], unit[:], gbv[:, ct:ct + 1],
                                                   ALU.mult, ALU.add)
                last.then_inc(S["res0_ready"], 1)

            nc.gpsimd.memset(ones[:], 1.0).then_inc(ones_ready, 1)
            nc.gpsimd.memset(neg_half[:], -0.5).then_inc(ones_ready, 1)
            nc.gpsimd.memset(unit[:], 1.0).then_inc(ones_ready, 1)
            wait(ones_ready, 3)
            wait(bias_ready, 1)
            wait(S["x_split"], 2)
            residual0(0)
            for half in range(HALVES):
                split_x(1, half)
            wait(S["bias_read"], 1)
            with pool.Fori(0, IMAGES - 2) as b:
                links[1] = b
                normalise(b)
                residual1(b)
                residual0(b + 1)
                for m in range(3):
                    split_value1(b, m)
                split_x(b + 2, 0)
                split_value1(b, 3)
                split_x(b + 2, 1)
            links[0], links[1] = links[0] + (IMAGES - 3) * LINKS, None
            for b in (IMAGES - 2, IMAGES - 1):
                normalise(b)
                residual1(b)
                if b < IMAGES - 1:
                    residual0(b + 1)
                for m in range(4):
                    split_value1(b, m)

        @block.tensor
        def _(pe):
            c = Counts()
            mm = nc.tensor.matmul

            def wait(name, n):
                pe.wait_ge(S[name], c.at(name, n))

            def weight_products():
                pe.wait_ge(weights_loaded, 16 * 12)
                for ct in range(CT):
                    for out, a, b in ((wqq_ps, wq_f, wk_f), (wpv_ps, wv_f, wp_f)):
                        for o in range(CT):
                            last = mm(out[:, ct], a[:, o, ct * P:(ct + 1) * P], b[:, o],
                                      start=o == 0, stop=o == CT - 1)
                last.then_inc(weights_ps, 1)

            def bias_products(out):
                value_b_ps, rowk_ps, query_b_ps = bias_places(out)
                for o in range(CT):
                    mm(value_b_ps[:, 0:C], bv_rows[:, o], wp_f[:, o], start=o == 0, stop=o == CT - 1)
                for j in range(2):
                    for o in range(CT):
                        mm(value_b_ps[:, C + j:C + j + 1], bq_rows[:, o], bk_s[:, o:o + 1],
                           start=o == 0, stop=o == CT - 1)
                for ct in range(CT):
                    for out, w, b in ((rowk_ps, wq_f, bk_s), (query_b_ps, wk_f, bq_s)):
                        for o in range(CT):
                            last = mm(out[:, ct:ct + 1], w[:, o, ct * P:(ct + 1) * P], b[:, o:o + 1],
                                      start=o == 0, stop=o == CT - 1)
                return last

            def all_weights():
                pe.wait_ge(weights_read, 3)

            def three(out, w_hi, w_lo, m_hi, m_lo, first, last):
                mm(out, w_hi, m_hi, start=first, stop=False)
                mm(out, w_hi, m_lo, start=False, stop=False)
                return mm(out, w_lo, m_hi, start=False, stop=last)

            def take(*place):
                if place in c.marks:
                    wait(*c.marks[place])

            def logits(layer, k, slot):
                take("slot", slot)
                rows = slice(k * P, (k + 1) * P)
                if k == 0:
                    name = ("qk_split", "query_split")[layer]
                    wait(name, c.n[name])
                for half in range(HALVES):
                    out = ring[:, slot, half * HALF:(half + 1) * HALF]
                    cols = slice(half * HALF, (half + 1) * HALF)
                    if layer == 0:
                        last = mm(out, q4[:, rows], k4[:, cols], start=True, stop=True)
                    else:
                        for ct in range(CT):
                            last = three(out, query_hi[:, ct, rows], query_lo[:, ct, rows],
                                         h_hi[:, ct, cols], h_lo[:, ct, cols], ct == 0, ct == CT - 1)
                last.then_inc(S["ring_ready"], 1)
                c.up("exp_done")
                c.mark(("slot", slot), "exp_done")

            def transposes(k):
                wait("p_ready", c.n["p_ready"] + 1)
                c.up("p_ready")
                if c.n["t_lo"] or c.turn is not None:
                    wait("t_lo", c.n["t_lo"])
                for st in range(TILES):
                    last = nc.tensor.transpose(pt_ps[:, st], prob[:, k % 2, st * P:(st + 1) * P], ident_s[:])
                last.then_inc(S["t_ready"], 1)
                c.up("t_lo")

            def values0(half, r, tiles):
                ct = r // 2
                if r == 0:
                    wait("value0_split", c.n["value0_split"])
                    wait("t_lo", tiles)
                if r % 2 == 0:
                    take("bank", ct)
                w = slice(ct * P, (ct + 1) * P)
                for st in range(4 * (r % 2), 4 * (r % 2) + 4):
                    last = three(pv_ps[:, ct], v0_hi[:, st, w], v0_lo[:, st, w], pt_hi[half][:, st],
                                 pt_lo[half][:, st], st == 0, st == TILES - 1)
                if r % 2:
                    last.then_inc(S["pv_ready"], 1)
                    c.up("pv_read")
                    c.mark(("bank", ct), "pv_read")

            def values1(half, r):
                if half == 0:
                    if r == 0:
                        for _ in range(4):
                            c.up("value1_split")
                        wait("value1_split", c.n["value1_split"])
                    c.up("p_split"), c.up("p_split")
                    wait("p_split", c.n["p_split"])
                keys = slice(half * PER_HALF, (half + 1) * PER_HALF)
                two = ((0, 2 * r), (1, 2 * r), (0, 2 * r + 1), (1, 2 * r + 1))
                if r == 3:
                    two = two[0::2] + two[1::2]
                for ct, k in two:
                    if k == 0:
                        take("bank", ct)
                    w = slice(ct * P, (ct + 1) * P)
                    j, cols = block_of(k)
                    last = three(pv_ps[:, ct], v1_hi[:, k, w], v1_lo[:, k, w], pt_hi[j][:, keys, cols],
                                 pt_lo[j][:, keys, cols], k == 0, k == TILES - 1)
                    if half == 1 and (ct, k) == (CT - 1, 0):
                        last.then_inc(S["block0_free"], 1)
                    if k == TILES - 1:
                        last.then_inc(S["pv_ready"], 1)
                        c.up("pv_read")
                        c.mark(("bank", ct), "pv_read")

            def project(kind, m, slot):
                out = ring[:, slot]
                reader = {"norm": "norm_read", "value1": "v1_full", "bias": "bias_read"}.get(kind, f"{kind}_split")
                if kind == "query":
                    if m == 0:
                        pe.wait_ge(S["h_split"], c.up("h_split"))
                    take("slot", slot)
                    for half in range(HALVES):
                        cols = slice(half * HALF, (half + 1) * HALF)
                        for ct in range(CT):
                            w = (slice(None), ct, slice(m * P, (m + 1) * P))
                            last = three(out[:, cols], wqq_hi[w], wqq_lo[w], h_hi[:, ct, cols],
                                         h_lo[:, ct, cols], ct == 0, ct == CT - 1)
                if kind == "value1":
                    take("slot", slot)
                    for j in range(2):
                        for ct in range(CT):
                            w = (slice(None), ct, slice((2 * m + j) * P, (2 * m + j + 1) * P))
                            last = three(out[:, j * HALF:j * HALF + VW], h_hi[w], h_lo[w], wpv_hi[:, ct],
                                         wpv_lo[:, ct], ct == 0, ct == CT - 1)
                if kind == "qk":
                    if c.n["x_split"] == 0:
                        pe.wait_ge(layer0_split, 1)
                    pe.wait_ge(S["x_split"], c.up("x_split"))
                    take("slot", slot)
                    cols = slice(m * HALF, (m + 1) * HALF)
                    for ct in range(CT):
                        last = three(out[:, 0:HALF], wqk_hi[:, ct], wqk_lo[:, ct], x_hi[:, ct, cols],
                                     x_lo[:, ct, cols], ct == 0, ct == CT - 1)
                if kind == "value0":
                    if c.n["value0_split"] == 0:
                        pe.wait_ge(layer0_split, 2)
                    take("slot", slot)
                    for j in range(2):
                        for ct in range(CT):
                            w = (slice(None), ct, slice((2 * m + j) * P, (2 * m + j + 1) * P))
                            last = three(out[:, j * C:(j + 1) * C], x_hi[w], x_lo[w], wv0_hi[:, ct],
                                         wv0_lo[:, ct], ct == 0, ct == CT - 1)
                if kind == "bias":
                    take("slot", slot)
                    last = bias_products(out)
                if kind == "norm":
                    if m == 0:
                        pe.wait_ge(S["stats_ready"], c.up("stats_ready"))
                    else:
                        wait("norm_read", c.n["norm_read"])
                    take("slot", slot)
                    last = mm(out[:, 0:CT], group_s[:], mean_var[:, :, 0] if m == 0 else spread[:],
                              start=True, stop=True)
                last.then_inc(S["ring_ready"], 1)
                c.up(reader)
                c.mark(("slot", slot), reader)

            def step(now):
                def values():
                    for layer, half, r in now.parts:
                        if layer == 0:
                            beyond = now.old == (0, (half + 1) * PER_HALF % TILES)
                            values0(half, r, c.n["t_lo"] - beyond)
                        else:
                            values1(half, r)

                if now.values_first:
                    values()
                if now.tile:
                    logits(*now.tile, now.slot["tile",])
                for item in now.items:
                    if item not in now.late:
                        project(*item, now.slot[item])
                if not now.values_first:
                    values()
                for item in now.late:
                    project(*item, now.slot[item])
                if now.previous and now.previous[0] == 0:
                    transposes(now.previous[1])

            run_steps(pe, c, step, {FIRST: weight_products, FIRST + PV_LAG: all_weights})

        @block.scalar
        def _(act):
            c = Counts()
            copy, activation = nc.scalar.copy, nc.scalar.activation

            def x_to_hi(half):
                cols = slice(half * HALF, (half + 1) * HALF)
                copy(x_hi[:, :, cols], x_in[:, :, cols]).then_inc(S["x_hi"], 1)
                c.up("x_hi")

            def transposed_hi(now):
                half, cols = block_of(now.old[1])
                if now.block0:
                    act.wait_ge(S["block0_free"], c.up("block0_free"))
                act.wait_ge(S["t_ready"], c.up("t_ready"))
                copy(pt_hi[half][:, :, cols], pt_ps[:]).then_inc(S["t_hi"], 1)

            def rows_hi(k, inverse):
                half, cols = block_of(k)
                if k % PER_HALF == 0:
                    act.wait_ge(S["pv_ready"], c.now("pv_ready"))
                act.wait_ge(S["inv_ready"], inverse)
                activation(pt_hi[half][:, :, cols], prob[:, k % 2].rearrange("p (m n) -> p m n", n=P),
                           ACT.Identity, scale=row_inv[:, k % 2:k % 2 + 1]).then_inc(S["p_hi"], 1)

            def step(now):
                if now.previous:
                    inverse = c.up("inv_ready")
                for layer, half, r in now.parts:
                    for _ in range(r % 2 if layer == 0 else CT * (r == 3)):
                        c.up("pv_ready")
                if now.previous and now.previous[0] == 1 and now.previous[1] > 0:
                    rows_hi(now.previous[1], inverse)
                if now.old and now.old[0] == 0 and now.hi_first:
                    transposed_hi(now)
                if now.previous and now.previous[0] == 0:
                    k = now.previous[1] % 2
                    act.wait_ge(S["inv_ready"], inverse)
                    activation(prob[:, k], prob[:, k], ACT.Identity,
                               scale=row_inv[:, k:k + 1]).then_inc(S["p_ready"], 1)
                if now.old and now.old[0] == 0 and not now.hi_first:
                    transposed_hi(now)
                if now.tile:
                    k, slot = now.tile[1], now.slot["tile",]
                    act.wait_ge(S["row_ready"], c.up("row_ready"))
                    activation(prob[:, k % 2], ring[:, slot], ACT.Exp, bias=neg_max[:, k % 2:k % 2 + 1],
                               accum_out=row_sum[:, k % 2:k % 2 + 1]).then_inc(S["exp_done"], 1)
                    c.up("ring_ready")
                for kind, m in now.items:
                    slot = now.slot[kind, m]
                    ready = c.up("ring_ready")
                    if kind in ("norm", "bias"):
                        continue
                    if kind == "value1":
                        act.wait_ge(S["v1_full"], c.up("v1_full"))
                        copy(v1_hi[:, 2 * m:2 * m + 2], v1_f[:, m % 2]).then_inc(S["v1_hi"], 1)
                        continue
                    act.wait_ge(S["ring_ready"], ready)
                    out = ring[:, slot]
                    if kind == "query":
                        last = activation(query_hi[:, m], out, ACT.Identity, bias=query_b[:, m:m + 1])
                    if kind == "value0":
                        last = copy(v0_hi[:, 2 * m:2 * m + 2],
                                    out[:, 0:HALF].rearrange("p (j n) -> p j n", j=2))
                    if kind == "qk":
                        cols = slice(m * HALF, (m + 1) * HALF)
                        activation(q4[0:64, cols], out[0:64, 0:HALF], ACT.Identity, bias=bqk_s[0:64])
                        activation(k4[0:32, cols], out[64:96, 0:HALF], ACT.Identity, bias=bqk_s[64:96])
                        last = activation(k4[96:128, cols], out[96:128, 0:HALF], ACT.Identity, bias=bqk_s[96:128])
                    last.then_inc(S["proj_hi"], 1)
                if now.previous == (1, 0):
                    rows_hi(0, inverse)
                for ct in now.h:
                    if ct == 0:
                        act.wait_ge(S["coef_ready"], c.up("coef_ready"))
                    activation(h_hi[:, ct], x1[:, ct], ACT.Identity, bias=norm_c[:, ct:ct + 1],
                               scale=norm_a[:, ct:ct + 1]).then_inc(S["h_hi"], 1)
                if now.load_x:
                    act.wait_ge(x_loaded, 8 * c.now("x_hi"))
                    x_to_hi(0)
                    x_to_hi(1)

            for half in range(HALVES):
                act.wait_ge(x0_loaded[half], 16)
                x_to_hi(half)
            run_steps(act, c, step)

        @block.vector
        def _(dve):
            c = Counts()
            V = nc.vector

            def link(ins):
                ins.then_inc(S["link"], 1)
                dve.wait_ge(S["link"], c.up("link"))

            def split(hi, lo, src, scale=1.0):
                link(V.tensor_scalar(hi, src, scale, None, ALU.mult))
                return V.scalar_tensor_tensor(lo, src, scale, hi.bitcast(F32), ALU.mult, ALU.subtract)

            scale = C ** -0.5

            def first_weights():
                dve.wait_ge(wqk_loaded, 16 * 3)
                split(wqk_hi[:], wqk_lo[:], wqk_f).then_inc(layer0_split, 1)
                for half in range(HALVES):
                    cols = slice(half * HALF, (half + 1) * HALF)
                    dve.wait_ge(S["x_hi"], half + 1)
                    V.tensor_tensor(x_lo[:, :, cols], x_in[:, :, cols], x_hi[:, :, cols].bitcast(F32),
                                    ALU.subtract).then_inc(S["x_split"], 1)
                dve.wait_ge(wv0_loaded, 16 * 3)
                V.tensor_scalar(gbv[:], bv0_s[:], gamma_s[:], None, ALU.mult).then_inc(bias_ready, 1)
                split(wv0_hi[:], wv0_lo[:], wv0_f).then_inc(layer0_split, 1)

            def query_weights():
                dve.wait_ge(weights_ps, 1)
                split(wqq_hi[:], wqq_lo[:], wqq_ps, scale).then_inc(weights_read, 1)

            def value_weights():
                dve.wait_ge(ones_ready, 3)
                for rows, b in ((bv_rows, bv_s), (bq_rows, bq_s)):
                    for ct in range(CT):
                        last = V.tensor_scalar(rows[:, ct], ones[:], b[:, ct:ct + 1], None, ALU.mult)
                last.then_inc(weights_read, 1)
                split(wpv_hi[:, :, 0:C], wpv_lo[:, :, 0:C], wpv_ps).then_inc(weights_read, 1)

            def biases(out):
                value_b_ps, rowk_ps, query_b_ps = bias_places(out)
                dve.wait_ge(S["ring_ready"], c.now("ring_ready"))
                for j in range(2):
                    split(wpv_hi[:, :, C + j], wpv_lo[:, :, C + j], rowk_ps, scale)
                V.tensor_scalar(query_b[:], query_b_ps, scale, None, ALU.mult)
                V.tensor_copy(value_b[:, 0:C], value_b_ps[:, 0:C])
                V.tensor_scalar(value_b[:, C:VW], value_b_ps[:, C:VW], scale, None,
                                ALU.mult).then_inc(S["bias_read"], 1)
                dve.wait_ge(S["bias_read"], 1)

            def value1(m, slot):
                dve.wait_ge(S["ring_ready"], c.now("ring_ready"))
                if m >= 2:
                    dve.wait_ge(S["value1_split"], c.at("value1_split", c.n["value1_split"] - 1))
                out = ring[:, slot].rearrange("p (j n) -> p j n", j=2)
                V.tensor_scalar(row_const[:, 2 * m:2 * m + 2], out[:, :, C], value_b[:, C:C + 1], None, ALU.add)
                for j in range(2):
                    last = V.tensor_tensor(v1_f[:, m % 2, j], out[:, j, 0:C], value_b[:, 0:C], ALU.add)
                last.then_inc(S["v1_full"], 1)
                c.up("v1_full"), c.up("value1_split")

            def project_lo(kind, m, slot):
                c.up("proj_hi")
                dve.wait_ge(S["proj_hi"], c.now("proj_hi"))
                out = ring[:, slot]
                if kind == "query":
                    last = V.scalar_tensor_tensor(query_lo[:, m], out, query_b[:, m:m + 1],
                                                  query_hi[:, m].bitcast(F32), ALU.add, ALU.subtract)
                if kind == "value0":
                    two = slice(2 * m, 2 * m + 2)
                    last = V.tensor_tensor(v0_lo[:, two], out[:, 0:HALF].rearrange("p (j n) -> p j n", j=2),
                                           v0_hi[:, two].bitcast(F32), ALU.subtract)
                if kind == "qk":
                    cols = slice(m * HALF, (m + 1) * HALF)
                    V.scalar_tensor_tensor(q4[64:128, cols], out[0:64, 0:HALF], bqk_s[0:64],
                                           q4[0:64, cols].bitcast(F32), ALU.add, ALU.subtract)
                    V.scalar_tensor_tensor(k4[32:64, cols], out[64:96, 0:HALF], bk0_s[:],
                                           k4[0:32, cols].bitcast(F32), ALU.add, ALU.subtract)
                    last = V.scalar_tensor_tensor(k4[64:96, cols], out[96:128, 0:HALF], bqk_s[96:128],
                                                  k4[96:128, cols].bitcast(F32), ALU.add, ALU.subtract)
                last.then_inc(S[f"{kind}_split"], 1)

            def norm(m, slot):
                dve.wait_ge(S["ring_ready"], c.now("ring_ready"))
                got = ring[:, slot, 0:CT]
                if m == 0:
                    V.tensor_copy(group_mean[:], got)
                    link(V.tensor_tensor(dev[:], mean_var[:, :, 0], got, ALU.subtract))
                    link(V.tensor_tensor(dev2[:], dev[:], dev[:], ALU.mult))
                    last = V.tensor_tensor(spread[:], dev2[:], mean_var[:, :, 1], ALU.add)
                else:
                    last = V.tensor_scalar(var_eps[:], got, EPS, None, ALU.add)
                last.then_inc(S["norm_read"], 1)

            def add_values(layer, half, ct):
                cols = slice(half * HALF, (half + 1) * HALF)
                dve.wait_ge(S["pv_ready"], c.up("pv_ready"))
                if layer == 0:
                    if half == 0 and ct == 0:
                        dve.wait_ge(S["res0_ready"], c.up("res0_ready"))
                    V.scalar_tensor_tensor(x1[:, ct, cols], pv_ps[:, ct], gamma_s[:], x1[:, ct, cols],
                                           ALU.mult, ALU.add).then_inc(S["pv_read"], 1)
                    dve.wait_ge(S["pv_read"], c.up("pv_read"))
                    link(V.bn_stats(bn[:, ct, half * 6:(half + 1) * 6], x1[:, ct, cols]))
                    if half == HALVES - 1 and ct == CT - 1:
                        dve.sem_inc(dve_passed, 1)
                        V.bn_aggr(mean_var[:, 0], bn[:, 0])
                        V.bn_aggr(mean_var[:, 1], bn[:, 1]).then_inc(S["stats_ready"], 1)
                else:
                    if half == 0 and ct == 0:
                        dve.wait_ge(S["res1_ready"], c.up("res1_ready"))
                    V.tensor_tensor(res1[:, ct, cols], pv_ps[:, ct], res1[:, ct, cols],
                                    ALU.add).then_inc(S["pv_read"], 1)
                    c.up("pv_read")

            def values_results(parts):
                for layer, half, r in parts:
                    if layer == 0 and r % 2:
                        add_values(0, half, r // 2)
                    if layer == 1 and r == 3:
                        for ct in range(CT):
                            add_values(1, half, ct)

            def transposed_lo(now):
                half, cols = block_of(now.old[1])
                dve.wait_ge(S["t_hi"], c.up("t_hi"))
                V.tensor_tensor(pt_lo[half][:, :, cols], pt_ps[:], pt_hi[half][:, :, cols].bitcast(F32),
                                ALU.subtract).then_inc(S["t_lo"], 1)

            def rows_lo(k):
                src = prob[:, k % 2].rearrange("p (m n) -> p m n", n=P)
                half, cols = block_of(k)
                hi, lo = pt_hi[half][:, :, cols], pt_lo[half][:, :, cols]
                dve.wait_ge(S["p_hi"], c.up("p_hi"))
                V.scalar_tensor_tensor(lo, src, row_inv[:, k % 2:k % 2 + 1], hi.bitcast(F32), ALU.mult,
                                       ALU.subtract).then_inc(S["p_split"], 1)

            def step(now):
                if now.previous:
                    k = now.previous[1] % 2
                    dve.wait_ge(S["exp_done"], c.up("exp_done"))
                    V.reciprocal(row_inv[:, k:k + 1], row_sum[:, k:k + 1]).then_inc(S["inv_ready"], 1)
                    dve.wait_ge(S["inv_ready"], c.up("inv_ready"))
                if now.values_first:
                    values_results(now.parts)
                if now.tile:
                    layer, k = now.tile
                    bias = neg_max[:, k % 2:k % 2 + 1]
                    dve.wait_ge(S["ring_ready"], c.up("ring_ready"))
                    src = ring[:, now.slot["tile",]]
                    if layer == 0:
                        max_of = V.tensor_reduce(bias, src, AX_X, ALU.max, negate=True)
                    else:
                        link(V.tensor_reduce(neg_raw[:, k % 2:k % 2 + 1], src, AX_X, ALU.max, negate=True))
                        max_of = V.tensor_scalar(bias, neg_raw[:, k % 2:k % 2 + 1], row_const[:, k:k + 1],
                                                 row_const[:, k:k + 1], ALU.subtract, ALU.add)
                    max_of.then_inc(S["row_ready"], 1)
                if now.old and now.old[0] == 0:
                    transposed_lo(now)
                if now.previous and now.previous[0] == 1 and now.previous[1] > 0:
                    rows_lo(now.previous[1])
                for kind, m in now.items:
                    slot = now.slot[kind, m]
                    c.up("ring_ready")
                    if kind == "norm":
                        norm(m, slot)
                    elif kind == "value1":
                        value1(m, slot)
                    elif kind == "bias":
                        biases(ring[:, slot])
                    else:
                        project_lo(kind, m, slot)
                if not now.values_first:
                    values_results(now.parts)
                if now.previous == (1, 0):
                    rows_lo(0)

            first_weights()
            run_steps(dve, c, step, {FIRST + 1: query_weights, FIRST + 2: value_weights})


def kernel(x, L0_conv_Wq, L0_conv_bq, L0_conv_Wk, L0_conv_bk, L0_conv_Wv, L0_conv_bv, L0_conv_gamma,
           L1_conv_norm_w, L1_conv_norm_b, L1_conv_q_w, L1_conv_q_b, L1_conv_k_w, L1_conv_k_b,
           L1_conv_v_w, L1_conv_v_b, L1_conv_proj_w, L1_conv_proj_b):
    import numpy as np
    import concourse.bacc as bacc
    from concourse.bass_utils import run_bass_kernel_spmd

    def plain(a):
        return np.ascontiguousarray(np.asarray(a))

    def column(b):
        return plain(np.asarray(b).reshape(-1, P).T)

    q, k = np.asarray(L0_conv_Wq), np.asarray(L0_conv_Wk)
    qb, kb = np.asarray(L0_conv_bq), np.asarray(L0_conv_bk)
    arrays = dict(
        x=plain(x).reshape(IMAGES, C, N),
        wqk_t=plain(np.concatenate([q, q, k, k]).T), bqk=plain(np.concatenate([qb, qb, kb, kb])[:, None]),
        bk0=plain(kb[:, None]), wv0_t=plain(np.asarray(L0_conv_Wv).T), bv0=column(L0_conv_bv),
        gamma=plain(np.broadcast_to(np.asarray(L0_conv_gamma), (P, 1))),
        norm_w=column(L1_conv_norm_w), norm_b=column(L1_conv_norm_b),
        wq=plain(L1_conv_q_w), bq=column(L1_conv_q_b), wk=plain(L1_conv_k_w), bk=column(L1_conv_k_b),
        wv=plain(L1_conv_v_w), bv=column(L1_conv_v_b), wp_t=plain(np.asarray(L1_conv_proj_w).T),
        bp=column(L1_conv_proj_b),
        ident=np.eye(P, dtype=np.float32),
        group=np.kron(np.eye(P // GROUP), np.full((GROUP, GROUP), 1 / GROUP)).astype(np.float32),
    )
    nc = bacc.Bacc("TRN2", target_bir_lowering=False, num_devices=1)
    args = {name: nc.dram_tensor(f"in_{name}", a.shape, mybir.dt.from_np(a.dtype), kind="ExternalInput").ap()
            for name, a in arrays.items()}
    args["y"] = nc.dram_tensor("out_y", (IMAGES, C, N), F32, kind="ExternalOutput").ap()
    build(nc, **args)
    run = run_bass_kernel_spmd(nc, [{f"in_{name}": a for name, a in arrays.items()}], core_ids=[0])
    return run.results[0]["out_y"].reshape(np.asarray(x).shape)
```
